# Optimizing a Trainium2 kernel written in Bass

```python
import numpy as np
import jax
import jax.numpy as jnp

def _softmax(x, axis=-1):
    return jax.nn.softmax(x, axis=axis)
def _gelu(x):
    return jax.nn.gelu(x, approximate=True)
def _silu(x):
    return jax.nn.silu(x)
def _sigmoid(x):
    return jax.nn.sigmoid(x)
def _layernorm(x, axis=-1, eps=1e-5):
    m = jnp.mean(x, axis=axis, keepdims=True)
    v = jnp.var(x, axis=axis, keepdims=True)
    return (x - m) / jnp.sqrt(v + eps)
def _scatter_add(tgt, idx, src, axis=0):
    return tgt.at[idx].add(src)
def _segment_sum(src, seg, n):
    return jax.ops.segment_sum(src, seg, n)

kernel_name = 'mk_metaformer_d1_conv_nhwc256_8ee2c2'

def setup_inputs(seed: int = 0):
    np.random.seed(seed)
    _w = jnp.asarray
    def _rec_inputs():
        import jax
        import jax.numpy as jnp
        _gk = jax.random.key(seed)
        x = -0.0006537 + 1.001 * jax.random.normal(jax.random.fold_in(_gk, 1), (4, 48, 48, 256), jnp.float32)
        return x
    x = _rec_inputs()
    def _L0_conv_setup():
        import jax, jax.numpy as jnp
        import jax.lax as lax
        import numpy as np

        def angle_transform(x, sin, cos):
            x1 = x[..., ::2]
            x2 = x[..., 1::2]
            rot = jnp.stack([-x2, x1], axis=-1).reshape(x.shape)
            return x * cos + rot * sin
        key = jax.random.key(seed)
        ks = jax.random.split(key, 14)
        B, H, W, C, nH = (4, 48, 48, 256, 8)
        d = C // nH
        N = H * W
        x = jax.random.normal(ks[0], (B, H, W, C), jnp.float32)
        sin = jax.random.uniform(ks[1], (H, W, d), jnp.float32, -1.0, 1.0)
        cos = jax.random.uniform(ks[2], (H, W, d), jnp.float32, -1.0, 1.0)
        mask = jax.random.normal(ks[3], (nH, N, N), jnp.float32) * 0.02
        w_scale = 0.02
        Wq = jax.random.normal(ks[4], (C, C), jnp.float32) * w_scale
        bq = jnp.zeros((C,), jnp.float32)
        Wk = jax.random.normal(ks[5], (C, C), jnp.float32) * w_scale
        bk = jnp.zeros((C,), jnp.float32)
        Wv = jax.random.normal(ks[6], (C, C), jnp.float32) * w_scale
        bv = jnp.zeros((C,), jnp.float32)
        dw_w = jax.random.normal(ks[7], (5, 5, 1, C), jnp.float32) * 0.05
        dw_b = jnp.zeros((C,), jnp.float32)
        Wo = jax.random.normal(ks[8], (C, C), jnp.float32) * w_scale
        bo = jnp.zeros((C,), jnp.float32)
        return {'x': x, 'sin': sin, 'cos': cos, 'mask': mask, 'Wq': Wq, 'bq': bq, 'Wk': Wk, 'bk': bk, 'Wv': Wv, 'bv': bv, 'dw_w': dw_w, 'dw_b': dw_b, 'Wo': Wo, 'bo': bo, 'num_heads': 8}
    _L0_conv_all = _L0_conv_setup()
    _L0_conv_in = {k: v for k, v in _L0_conv_all.items() if k in ('sin', 'cos', 'mask', 'Wq', 'bq', 'Wk', 'bk', 'Wv', 'bv', 'dw_w', 'dw_b', 'Wo', 'bo', )}
    del _L0_conv_all

    def _L0_ffn_setup():
        import jax, jax.numpy as jnp
        import numpy as np
        B, N, D = (16, 4096, 256)
        NUM_EXPERTS, TOP_K, HEADS = (4, 2, 4)
        N_EDGES = 1048576
        LN_EPS = 1e-05

        def _layernorm(x, g, b):
            mu = x.mean(-1, keepdims=True)
            var = ((x - mu) ** 2).mean(-1, keepdims=True)
            return (x - mu) * jax.lax.rsqrt(var + LN_EPS) * g + b

        def _forward(x, edge_index, W_gat, att_src, att_dst, b_gat, ln_gamma, ln_beta, W1, b1, W2, b2):
            Bc, Nc, Dc = x.shape
            M = Bc * Nc
            x_flat = x.reshape(M, Dc)
            h = (x_flat @ W_gat).reshape(M, HEADS, NUM_EXPERTS)
            loops = jnp.arange(M, dtype=edge_index.dtype)
            src = jnp.concatenate([edge_index[0], loops])
            dst = jnp.concatenate([edge_index[1], loops])
            a_src = (h * att_src).sum(-1)
            a_dst = (h * att_dst).sum(-1)
            e = jax.nn.leaky_relu(a_src[src] + a_dst[dst], negative_slope=0.2)
            e_max = jax.ops.segment_max(e, dst, num_segments=M)
            ee = jnp.exp(e - e_max[dst])
            denom = jax.ops.segment_sum(ee, dst, num_segments=M)
            alpha = ee / (denom[dst] + 1e-16)
            msg = h[src] * alpha[:, :, None]
            agg = jax.ops.segment_sum(msg, dst, num_segments=M).reshape(M, HEADS * NUM_EXPERTS) + b_gat
            scores = _layernorm(agg, ln_gamma, ln_beta).reshape(M, HEADS, NUM_EXPERTS).mean(1)
            scores = scores.reshape(Bc, Nc, NUM_EXPERTS)
            topk_s, topk_i = jax.lax.top_k(scores, TOP_K)
            w = jax.nn.softmax(topk_s, axis=-1)
            out = jnp.zeros_like(x)
            for ei in range(NUM_EXPERTS):
                g = jnp.where(topk_i == ei, w, 0.0).sum(-1)
                hh = jax.nn.gelu(x @ W1[ei] + b1[ei], approximate=False)
                out = out + g[..., None] * (hh @ W2[ei] + b2[ei])
            return out
        key = jax.random.key(seed)
        ks = jax.random.split(key, 8)
        s = 0.05
        return {'x': jax.random.normal(ks[0], (B, N, D), jnp.float32), 'W_gat': jax.random.normal(ks[1], (D, HEADS * NUM_EXPERTS), jnp.float32) * s, 'att_src': jax.random.normal(ks[2], (HEADS, NUM_EXPERTS), jnp.float32) * s, 'att_dst': jax.random.normal(ks[3], (HEADS, NUM_EXPERTS), jnp.float32) * s, 'b_gat': jnp.zeros((HEADS * NUM_EXPERTS,), jnp.float32), 'ln_gamma': jnp.ones((HEADS * NUM_EXPERTS,), jnp.float32), 'ln_beta': jnp.zeros((HEADS * NUM_EXPERTS,), jnp.float32), 'W1': jax.random.normal(ks[4], (NUM_EXPERTS, D, 2 * D), jnp.float32) * s, 'b1': jnp.zeros((NUM_EXPERTS, 2 * D), jnp.float32), 'W2': jax.random.normal(ks[5], (NUM_EXPERTS, 2 * D, D), jnp.float32) * s, 'b2': jnp.zeros((NUM_EXPERTS, D), jnp.float32), 'edge_index': jax.random.randint(ks[6], (2, N_EDGES), 0, B * N, jnp.int32)}
    _L0_ffn_all = _L0_ffn_setup()
    _L0_ffn_in = {k: v for k, v in _L0_ffn_all.items() if k in ('W_gat', 'att_src', 'att_dst', 'b_gat', 'ln_gamma', 'ln_beta', 'W1', 'b1', 'W2', 'b2', 'edge_index', )}
    del _L0_ffn_all

    return {
        "x": x,
        "L0_conv_sin": _L0_conv_in["sin"],
        "L0_conv_cos": _L0_conv_in["cos"],
        "L0_conv_mask": _L0_conv_in["mask"],
        "L0_conv_Wq": _L0_conv_in["Wq"],
        "L0_conv_bq": _L0_conv_in["bq"],
        "L0_conv_Wk": _L0_conv_in["Wk"],
        "L0_conv_bk": _L0_conv_in["bk"],
        "L0_conv_Wv": _L0_conv_in["Wv"],
        "L0_conv_bv": _L0_conv_in["bv"],
        "L0_conv_dw_w": _L0_conv_in["dw_w"],
        "L0_conv_dw_b": _L0_conv_in["dw_b"],
        "L0_conv_Wo": _L0_conv_in["Wo"],
        "L0_conv_bo": _L0_conv_in["bo"],
        "L0_ffn_W_gat": _L0_ffn_in["W_gat"],
        "L0_ffn_att_src": _L0_ffn_in["att_src"],
        "L0_ffn_att_dst": _L0_ffn_in["att_dst"],
        "L0_ffn_b_gat": _L0_ffn_in["b_gat"],
        "L0_ffn_ln_gamma": _L0_ffn_in["ln_gamma"],
        "L0_ffn_ln_beta": _L0_ffn_in["ln_beta"],
        "L0_ffn_W1": _L0_ffn_in["W1"],
        "L0_ffn_b1": _L0_ffn_in["b1"],
        "L0_ffn_W2": _L0_ffn_in["W2"],
        "L0_ffn_b2": _L0_ffn_in["b2"],
        "L0_ffn_edge_index": _L0_ffn_in["edge_index"],
    }

def reference(x, L0_conv_sin, L0_conv_cos, L0_conv_mask, L0_conv_Wq, L0_conv_bq, L0_conv_Wk, L0_conv_bk, L0_conv_Wv, L0_conv_bv, L0_conv_dw_w, L0_conv_dw_b, L0_conv_Wo, L0_conv_bo, L0_ffn_W_gat, L0_ffn_att_src, L0_ffn_att_dst, L0_ffn_b_gat, L0_ffn_ln_gamma, L0_ffn_ln_beta, L0_ffn_W1, L0_ffn_b1, L0_ffn_W2, L0_ffn_b2, L0_ffn_edge_index):
    import jax
    import jax.numpy as jnp
    def _L0_conv_ref(x, sin, cos, mask, Wq, bq, Wk, bk, Wv, bv, dw_w, dw_b, Wo, bo, num_heads):
        import jax, jax.numpy as jnp
        import jax.lax as lax
        import numpy as np

        def angle_transform(x, sin, cos):
            x1 = x[..., ::2]
            x2 = x[..., 1::2]
            rot = jnp.stack([-x2, x1], axis=-1).reshape(x.shape)
            return x * cos + rot * sin
        B, H, W, C = x.shape
        d = C // num_heads
        N = H * W
        scaling = d ** (-0.5)
        q = x @ Wq + bq
        k = (x @ Wk + bk) * scaling
        v = x @ Wv + bv
        lepe = lax.conv_general_dilated(v, dw_w, window_strides=(1, 1), padding=((2, 2), (2, 2)), dimension_numbers=('NHWC', 'HWIO', 'NHWC'), feature_group_count=C) + dw_b
        qh = q.reshape(B, H, W, num_heads, d).transpose(0, 3, 1, 2, 4)
        kh = k.reshape(B, H, W, num_heads, d).transpose(0, 3, 1, 2, 4)
        vh = v.reshape(B, H, W, num_heads, d).transpose(0, 3, 1, 2, 4)
        qr = angle_transform(qh, sin, cos).reshape(B, num_heads, N, d)
        kr = angle_transform(kh, sin, cos).reshape(B, num_heads, N, d)
        vr = vh.reshape(B, num_heads, N, d)
        attn = jnp.einsum('bhnd,bhmd->bhnm', qr, kr) + mask
        out = jnp.einsum('bhnm,bhmd->bhnd', jax.nn.softmax(attn, axis=-1), vr)
        out = out.transpose(0, 2, 1, 3).reshape(B, H, W, C)
        out = out + lepe
        return out @ Wo + bo

    def _L0_ffn_ref(x, W_gat, att_src, att_dst, b_gat, ln_gamma, ln_beta, W1, b1, W2, b2, edge_index):
        import jax, jax.numpy as jnp
        import numpy as np
        B, N, D = (16, 4096, 256)
        NUM_EXPERTS, TOP_K, HEADS = (4, 2, 4)
        N_EDGES = 1048576
        LN_EPS = 1e-05

        def _layernorm(x, g, b):
            mu = x.mean(-1, keepdims=True)
            var = ((x - mu) ** 2).mean(-1, keepdims=True)
            return (x - mu) * jax.lax.rsqrt(var + LN_EPS) * g + b

        def _forward(x, edge_index, W_gat, att_src, att_dst, b_gat, ln_gamma, ln_beta, W1, b1, W2, b2):
            Bc, Nc, Dc = x.shape
            M = Bc * Nc
            x_flat = x.reshape(M, Dc)
            h = (x_flat @ W_gat).reshape(M, HEADS, NUM_EXPERTS)
            loops = jnp.arange(M, dtype=edge_index.dtype)
            src = jnp.concatenate([edge_index[0], loops])
            dst = jnp.concatenate([edge_index[1], loops])
            a_src = (h * att_src).sum(-1)
            a_dst = (h * att_dst).sum(-1)
            e = jax.nn.leaky_relu(a_src[src] + a_dst[dst], negative_slope=0.2)
            e_max = jax.ops.segment_max(e, dst, num_segments=M)
            ee = jnp.exp(e - e_max[dst])
            denom = jax.ops.segment_sum(ee, dst, num_segments=M)
            alpha = ee / (denom[dst] + 1e-16)
            msg = h[src] * alpha[:, :, None]
            agg = jax.ops.segment_sum(msg, dst, num_segments=M).reshape(M, HEADS * NUM_EXPERTS) + b_gat
            scores = _layernorm(agg, ln_gamma, ln_beta).reshape(M, HEADS, NUM_EXPERTS).mean(1)
            scores = scores.reshape(Bc, Nc, NUM_EXPERTS)
            topk_s, topk_i = jax.lax.top_k(scores, TOP_K)
            w = jax.nn.softmax(topk_s, axis=-1)
            out = jnp.zeros_like(x)
            for ei in range(NUM_EXPERTS):
                g = jnp.where(topk_i == ei, w, 0.0).sum(-1)
                hh = jax.nn.gelu(x @ W1[ei] + b1[ei], approximate=False)
                out = out + g[..., None] * (hh @ W2[ei] + b2[ei])
            return out
        return _forward(x, edge_index, W_gat, att_src, att_dst, b_gat, ln_gamma, ln_beta, W1, b1, W2, b2)

    def _gn(v, G=32, eps=1e-5):
        B_, H_, W_, C_ = v.shape
        g = v.reshape(B_, H_, W_, G, C_ // G)
        m = jnp.mean(g, axis=(1, 2, 4), keepdims=True)
        s = jnp.var(g, axis=(1, 2, 4), keepdims=True)
        return ((g - m) / jnp.sqrt(s + eps)).reshape(v.shape)

    def _ln_c(v, eps=1e-6):
        m = jnp.mean(v, axis=-1, keepdims=True)
        s = jnp.var(v, axis=-1, keepdims=True)
        return (v - m) / jnp.sqrt(s + eps)

    def _ln_t(v, eps=1e-5):
        m = jnp.mean(v, axis=-1, keepdims=True)
        s = jnp.var(v, axis=-1, keepdims=True)
        return (v - m) / jnp.sqrt(s + eps)

    def _to_tokens(v):
        B_, H_, W_, C_ = v.shape
        return v.reshape(B_, H_ * W_, C_)
    def _from_tokens(t, like):
        return t.reshape(like.shape)

    x = x + _L0_conv_ref(_ln_c(x), L0_conv_sin, L0_conv_cos, L0_conv_mask, L0_conv_Wq, L0_conv_bq, L0_conv_Wk, L0_conv_bk, L0_conv_Wv, L0_conv_bv, L0_conv_dw_w, L0_conv_dw_b, L0_conv_Wo, L0_conv_bo, 8)
    t = _to_tokens(x)
    t = t + _L0_ffn_ref(_ln_t(t), L0_ffn_W_gat, L0_ffn_att_src, L0_ffn_att_dst, L0_ffn_b_gat, L0_ffn_ln_gamma, L0_ffn_ln_beta, L0_ffn_W1, L0_ffn_b1, L0_ffn_W2, L0_ffn_b2, L0_ffn_edge_index)
    x = _from_tokens(t, x)
    return x


_drawn_inputs = setup_inputs


def setup_inputs(seed=0):
    import zlib

    import numpy as np

    out = dict(_drawn_inputs(seed))
    spreads = {'L0_conv_bq': (0.0, 0.8),
     'L0_conv_bk': (0.0, 0.8),
     'L0_conv_bv': (0.0, 0.1),
     'L0_conv_dw_b': (0.0, 0.1),
     'L0_conv_bo': (0.0, 0.1),
     'L0_ffn_b_gat': (0.0, 0.1),
     'L0_ffn_ln_gamma': (1.0, 0.562),
     'L0_ffn_ln_beta': (0.0, 0.438),
     'L0_ffn_b1': (0.0, 0.1),
     'L0_ffn_b2': (0.0, 0.1)}
    factors = {'L0_conv_sin': 8.0,
     'L0_conv_cos': 8.0,
     'L0_conv_Wq': 8.0,
     'L0_conv_Wk': 8.0,
     'L0_ffn_att_src': 8.0,
     'L0_ffn_att_dst': 8.0}
    for name, (base, spread) in spreads.items():
        noise = np.random.default_rng([zlib.crc32(name.encode()), seed]).standard_normal(out[name].shape)
        drawn = base * np.exp(spread * noise) if base else spread * noise
        out[name] = jnp.asarray(drawn.astype(out[name].dtype))
    for name, factor in factors.items():
        out[name] = (out[name] * factor).astype(out[name].dtype)
    return out
```

```python
from contextlib import ExitStack

import numpy as np

import concourse.bass as bass
from concourse import mybir

F32 = mybir.dt.float32
F16 = mybir.dt.float16
BF16 = mybir.dt.bfloat16
I32 = mybir.dt.int32
U32 = mybir.dt.uint32
ALU = mybir.AluOpType
ACT = mybir.ActivationFunctionType
AX = mybir.AxisListType
REDUCE_MAX = bass.bass_isa.ReduceOp.max

B, H, W, C = 4, 48, 48, 256
NH, HD = 8, 32
N = H * W
M = B * N
P = 128
CC = C // P
TG = 3
GT = TG * P
GI = N // GT
NG = M // GT
GR = GT // W
PH, PW = H + 4, W + 4
VS = 3 * HD
V_SCALE = 64.0
P_SHIFT = 14 * float(np.log(2.0))
JM = N // P

NX, GF, GHD = 4, 512, 4
HF = GHD * NX
TR = HF + GHD
E = 1048576
EC = E // P
ET = 16
LO, HI = 6, 1536
NTILE = M // P
LN_EPS = 1e-5


class Steps:

    def __init__(self, eng, sem, start=0):
        self.eng, self.sem, self.start, self.n = eng, sem, start, 0

    def __call__(self, ins, lag=0):
        self.mark(ins)
        if self.n > lag:
            self.eng.wait_ge(self.sem, self.start + self.n - lag)

    def mark(self, ins):
        self.n += 1
        ins.then_inc(self.sem, 1)

    def wait(self):
        self.eng.wait_ge(self.sem, self.start + self.n)


class Space:

    def __init__(self, nc, ctx, tag):
        self.nc, self.ctx, self.tag = nc, ctx, tag

    def sb(self, name, shape, dt=F32):
        return self.ctx.enter_context(self.nc.sbuf_tensor(f"{self.tag}_{name}", shape, dt))

    def ps(self, name, shape, dt=F32):
        return self.ctx.enter_context(self.nc.psum_tensor(f"{self.tag}_{name}", shape, dt))

    def sem(self, name):
        return self.ctx.enter_context(self.nc.semaphore(f"{self.tag}_{name}"))


def make_identity(pool, ident, sem):
    pool.memset(ident[:, :], 0.0).then_inc(sem, 1)
    pool.wait_ge(sem, 1)
    pool.affine_select(out=ident[:, :], in_=ident[:, :], compare_op=ALU.not_equal, fill=1.0,
                       base=0, pattern=[[-1, P]], channel_multiplier=1).then_inc(sem, 1)


def part_wait(eng, passed):
    eng.sem_inc(passed, 1)


def layernorm_stats(dve, step, x_tiles, stats, mean_var, tiles, passed):
    for t in range(tiles):
        step.mark(dve.bn_stats(stats[:, t, :], x_tiles[:, t, :]))
    step.wait()
    part_wait(dve, passed)
    for t in range(tiles):
        step.mark(dve.bn_aggr(mean_var[:, t, :], stats[:, t, :]))
    step.wait()


def reciprocal_root(dve, step, root, var, tmp, eps):
    step(dve.reciprocal(root[:, :], root[:, :]))
    step(dve.tensor_tensor(tmp[:, :], root[:, :], root[:, :], ALU.mult))
    step(dve.scalar_tensor_tensor(out=tmp[:, :], in0=var, scalar=eps, in1=tmp[:, :], op0=ALU.add, op1=ALU.mult))
    step(dve.tensor_scalar(tmp[:, :], tmp[:, :], -0.5, 1.5, ALU.mult, ALU.add))
    step(dve.tensor_tensor(root[:, :], root[:, :], tmp[:, :], ALU.mult))


def project_qkv(nc, a, scr):
    ctx = ExitStack()
    with ctx:
        s = Space(nc, ctx, "qkv")
        x_in = [s.sb(f"x_in{i}", [P, TG, C]) for i in range(2)]
        x_norm = [s.sb(f"x_norm{i}", [P, TG, C]) for i in range(2)]
        stats = s.sb("stats", [P, TG, 6])
        mean_var = s.sb("mean_var", [P, TG, 2])
        rstd = s.sb("rstd", [P, TG])
        newton = s.sb("newton", [P, TG])
        ident = s.sb("ident", [P, P])
        xT = s.sb("xT", [P, CC, GT])
        w = [s.sb(f"w{i}", [P, CC, C]) for i in range(5)]
        bias = s.sb("bias", [P, 5, CC])
        bv_row = s.sb("bv_row", [P, C])
        cos = s.sb("cos", [P, N])
        sin = s.sb("sin", [P, N])
        sign = s.sb("sign", [P, 1])
        eps = s.sb("eps", [P, 1])
        lin = s.sb("lin", [P, 4, CC, GT])
        turned = [s.sb(f"turned{i}", [P, CC, GT]) for i in range(2)]
        tmp = s.sb("tmp", [P, CC, GT])
        hi = [[s.sb(f"hi{i}{j}", [P, CC, GT], F16) for j in range(2)] for i in range(2)]
        lo = [[s.sb(f"lo{i}{j}", [P, CC, GT], F16) for j in range(2)] for i in range(2)]
        v_chan = [s.sb(f"v_chan{i}", [P, CC, GT]) for i in range(2)]
        v_tok = s.sb("v_tok", [P, TG, C])
        v_stack = [s.sb(f"v_stack{i}", [P, TG, NH, VS], F16) for i in range(2)]
        zeros = s.sb("zeros", [P, CC, PH * PW])
        t_ps = s.ps("t_ps", [P, CC, 512])
        o_ps = s.ps("o_ps", [P, 6, 512])

        const_in = s.sem("const_in")
        const_ok = s.sem("const_ok")
        act_const = s.sem("act_const")
        ident_ok = s.sem("ident_ok")
        x_ready = [s.sem(f"x_ready{i}") for i in range(2)]
        x_free = s.sem("x_free")
        stats_ok = s.sem("stats_ok")
        root_ok = s.sem("root_ok")
        norm_ok = s.sem("norm_ok")
        norm_free = s.sem("norm_free")
        turn_done = s.sem("turn_done")
        xT_ok = s.sem("xT_ok")
        lin_done = s.sem("lin_done")
        lin_taken = s.sem("lin_taken")
        v_rows_taken = s.sem("v_rows_taken")
        turned_ok = s.sem("turned_ok")
        hi_ok = s.sem("hi_ok")
        parts_ok = s.sem("parts_ok")
        turned_free = s.sem("turned_free")
        lin_free = s.sem("lin_free")
        v_tok_ok = s.sem("v_tok_ok")
        v_hi_ok = s.sem("v_hi_ok")
        v_ok = s.sem("v_ok")
        stored = [s.sem(f"stored{i}") for i in range(2)]
        zeroed = s.sem("zeroed")
        dve_s = s.sem("dve_s")
        passed = s.sem("passed")

        x_v = a["x"].rearrange("(g t p) c -> g p t c", t=TG, p=P)
        NCONST = 5 + 5 + 1 + 8 + 1
        STORES = 8 * CC + CC + TG
        DVE_PER = 2 * TG + 5

        block = ctx.enter_context(nc.Block())

        @block.sync
        def _(sp):
            for par in range(2):
                sp.sem_inc(stored[par], 16)
            for i, n in enumerate(["Wq", "Wq_swap", "Wk", "Wk_swap", "Wv"]):
                sp.dma_start(w[i][:, :, :], a[n].rearrange("(k p) n -> p k n", p=P)).then_inc(const_in, 16)
            for i, n in enumerate(["bq", "bq_swap", "bk", "bk_swap", "bv"]):
                sp.dma_start(bias[:, i, :], a[n]).then_inc(const_in, 16)
            sp.dma_start(bv_row[:, :], a["bv_row"].to_broadcast([P, C])).then_inc(const_in, 16)
            for r in range(P // HD):
                sp.dma_start(cos[r * HD:(r + 1) * HD, :], a["cos"]).then_inc(const_in, 16)
                sp.dma_start(sin[r * HD:(r + 1) * HD, :], a["sin"]).then_inc(const_in, 16)
            sp.dma_start(sign[:, :], a["sign"]).then_inc(const_in, 16)
            sp.wait_ge(zeroed, 1)
            for b in range(B):
                sp.dma_start(scr["v_pad"].rearrange("(m p) b n -> b p m n", p=P)[b], zeros[:, :, :]).then_inc(zeroed, 16)
            sp.wait_ge(zeroed, 1 + 16 * B)
            sp.wait_ge(ident_ok, 4)
            with sp.Fori(0, B) as b:
                with sp.Fori(0, GI // 2) as gp:
                    for par in range(2):
                        g = b * GI + gp * 2 + par
                        tok = g * GT
                        for i, name in enumerate(["q_parts", "k_parts"]):
                            dst = scr[name].rearrange("(m h) (s d) n -> s m h d n", m=CC, d=HD)
                            sp.wait_ge(parts_ok, 2 * g + i + 1)
                            for sl, part in enumerate([hi, hi, lo, lo] if i == 0 else [hi, lo, hi, lo]):
                                for m in range(CC):
                                    sp.dma_start(dst[sl, m, :, :, bass.ds(tok, GT)], part[i][par][:, m, :])\
                                        .then_inc(stored[par], 16)
                        sp.wait_ge(v_ok, g + 1)
                        dst = scr["v_pad"].rearrange("(m p) b (r w) -> m p b r w", p=P, w=PW)
                        for m in range(CC):
                            sp.dma_start(dst[m, :, b, bass.ds(gp * 2 * GR + par * GR + 2, GR), 2:2 + W],
                                           v_chan[par][:, m, :].rearrange("p (r w) -> p r w", w=W))\
                                .then_inc(stored[par], 16)
                        dst = scr["v_stack"].rearrange("b h p (g k) -> b g p h k", k=TG * VS)
                        for t in range(TG):
                            sp.dma_start(dst[b, gp * 2 + par, :, :, t * VS:(t + 1) * VS],
                                           v_stack[par][:, t, :, :]).then_inc(stored[par], 16)
            for par in range(2):
                sp.wait_ge(stored[par], 16 + 16 * STORES * NG // 2)

        @block.gpsimd
        def _(pool):
            make_identity(pool, ident, ident_ok)
            for i in range(2):
                pool.memset(v_stack[i][:, :, :, 2 * HD:], 1.0).then_inc(ident_ok, 1)
            with pool.Fori(0, NG // 2) as i:
                for par in range(2):
                    pool.wait_ge(x_free, 2 * i + par + 1)
                    pool.dma_start(x_in[par][:, :, :], x_v[2 * i + par]).then_inc(x_ready[par], 16)
            pool.wait_ge(x_free, NG + 1)
            pool.dma_start(x_in[0][:, :, :], x_v[0]).then_inc(x_ready[0], 16)

        @block.tensor
        def _(pe):
            pe.wait_ge(ident_ok, 2)
            pe.wait_ge(const_in, 16 * NCONST)
            pe.sem_inc(norm_free, 2)
            pe.sem_inc(lin_done, 12)
            with pe.Fori(0, NG // 2) as i:
                for par in range(2):
                    g = 2 * i + par
                    pe.wait_ge(norm_ok, g + 1)
                    pe.wait_ge(xT_ok, 2 + 2 * g)
                    for t in range(TG):
                        for m in range(CC):
                            last = pe.transpose(t_ps[:, m, t * P:(t + 1) * P], x_norm[par][:, t, m * P:(m + 1) * P],
                                                ident[:, :])
                    last.then_inc(turn_done, 1)
                    pe.wait_ge(turn_done, g + 1)
                    pe.sem_inc(norm_free, 1)
                    pe.wait_ge(xT_ok, 2 + 2 * g + 2)
                    for n in range(12):
                        bank = [0, 1, 2, 3, 0, 1, 2, 3, 4, 5, 4, 5][n]
                        if n < 8:
                            pe.wait_ge(lin_taken, 8 * g + 8 + n - 4 + 1)
                        else:
                            pe.wait_ge(v_rows_taken, 4 * g + 4 + n - 8 - 2 + 1)
                        if n < 10:
                            wi, m = (n % 4, n // 4) if n < 8 else (4, n - 8)
                            for k in range(CC):
                                last = pe.matmul(o_ps[:, bank, :GT], w[wi][:, k, m * P:(m + 1) * P], xT[:, k, :],
                                                 start=(k == 0), stop=(k == CC - 1))
                        else:
                            for t in ([0, 1] if n == 10 else [2]):
                                for k in range(CC):
                                    last = pe.matmul(o_ps[:, bank, (t % 2) * C:(t % 2 + 1) * C],
                                                     xT[:, k, t * P:(t + 1) * P], w[4][:, k, :],
                                                     start=(k == 0), stop=(k == CC - 1))
                        last.then_inc(lin_done, 1)

        @block.scalar
        def _(act):
            act.sem_inc(lin_taken, 8)
            act.sem_inc(xT_ok, 2)
            act.wait_ge(const_ok, 2)
            act.mul(bias[:, 2:4, :], bias[:, 2:4, :], HD ** -0.5).then_inc(act_const, 1)
            act.wait_ge(act_const, 1)
            act.wait_ge(stats_ok, 1)
            act.activation(rstd[:, :], mean_var[:, :, 1], ACT.Sqrt, bias=eps[:, :]).then_inc(root_ok, 1)
            with act.Fori(0, NG // 2) as i:
                for par in range(2):
                    g = 2 * i + par
                    act.wait_ge(stats_ok, g + 2)
                    act.activation(rstd[:, :], mean_var[:, :, 1], ACT.Sqrt, bias=eps[:, :]).then_inc(root_ok, 1)
                    act.wait_ge(turn_done, g + 1)
                    for m in range(CC):
                        if m == 0:
                            act.wait_ge(lin_done, 12 + 12 * g)
                        act.activation(xT[:, m, :], t_ps[:, m, :GT], ACT.Identity).then_inc(xT_ok, 1)
                    for n in range(8):
                        wi, m = n % 4, n // 4
                        act.wait_ge(lin_done, 12 + 12 * g + n + 1)
                        if n == 0:
                            act.wait_ge(lin_free, 2 + 2 * g)
                        act.activation(lin[:, wi, m, :], o_ps[:, wi, :GT], ACT.Identity, bias=bias[:, wi, m:m + 1],
                                       scale=1.0 if wi < 2 else HD ** -0.5).then_inc(lin_taken, 1)
                    act.wait_ge(stored[par], 16 + 16 * STORES * i)
                    for m in range(CC):
                        act.wait_ge(lin_done, 12 + 12 * g + 9 + m)
                        act.activation(v_chan[par][:, m, :], o_ps[:, 4 + m, :GT], ACT.Identity,
                                       bias=bias[:, 4, m:m + 1]).then_inc(v_rows_taken, 1)
                    for n in range(2):
                        act.wait_ge(turned_ok, 2 * g + n + 1)
                        act.activation(hi[n][par][:, :, :], turned[n][:, :, :], ACT.Identity).then_inc(hi_ok, 1)
                    act.wait_ge(v_tok_ok, g + 1)
                    act.activation(v_stack[par][:, :, :, 0:HD], v_tok[:, :, :].rearrange("p t (h d) -> p t h d", d=HD),
                                   ACT.Identity, scale=V_SCALE).then_inc(v_hi_ok, 1)

        @block.vector
        def _(dve):
            step = Steps(dve, dve_s)
            dve.sem_inc(x_free, 2)
            dve.sem_inc(lin_free, 2)
            dve.sem_inc(v_rows_taken, 4)
            dve.memset(zeros[:, :, :], 0.0).then_inc(zeroed, 1)
            dve.wait_ge(const_in, 16 * NCONST)
            dve.memset(eps[:, :], 1e-6).then_inc(const_ok, 1)
            dve.tensor_scalar(sin[:, :], sin[:, :], sign[:, 0:1], None, ALU.mult).then_inc(const_ok, 1)
            dve.wait_ge(const_ok, 2)

            def normalise(g, i, par, started):
                step.start, step.n = started, 0
                dve.wait_ge(x_ready[par], 16 * i + 16)
                layernorm_stats(dve, step, x_in[par], stats, mean_var, TG, passed)
                dve.sem_inc(stats_ok, 1)
                dve.wait_ge(root_ok, g + 1)
                reciprocal_root(dve, step, rstd, mean_var[:, :, 1], newton, 1e-6)
                dve.wait_ge(norm_free, g + 1)
                for t in range(TG):
                    last = dve.tensor_scalar(x_norm[par][:, t, :], x_in[par][:, t, :], mean_var[:, t, 0:1],
                                             rstd[:, t:t + 1], ALU.subtract, ALU.mult)
                last.then_inc(norm_ok, 1)
                dve.wait_ge(norm_ok, g + 1)
                dve.sem_inc(x_free, 1)

            normalise(0, 0, 0, 0)
            with dve.Fori(0, B) as b:
                with dve.Fori(0, GI // 2) as gp:
                    for par in range(2):
                        i = b * (GI // 2) + gp
                        g = 2 * i + par
                        normalise(g + 1, i + par, 1 - par, (g + 1) * DVE_PER + g * 5)
                        step.start, step.n = (g + 2) * DVE_PER + g * 5, 0
                        here = bass.ds(gp * 2 * GT + par * GT, GT)
                        dve.wait_ge(stored[par], 16 + 16 * STORES * i)
                        for n in range(2):
                            dve.wait_ge(lin_taken, 8 * g + 8 + 6 + 2 * n)
                            dve.tensor_tensor(tmp[:, :, :], lin[:, 2 * n + 1, :, :],
                                              sin[:, None, here].to_broadcast([P, CC, GT]), ALU.mult)
                            step(dve.tensor_tensor(turned[n][:, :, :], lin[:, 2 * n, :, :],
                                                   cos[:, None, here].to_broadcast([P, CC, GT]), ALU.mult))
                            dve.tensor_tensor(turned[n][:, :, :], turned[n][:, :, :], tmp[:, :, :],
                                              ALU.add).then_inc(turned_ok, 1)
                            dve.wait_ge(turned_ok, 2 * g + n + 1)
                            dve.sem_inc(lin_free, 1)
                        dve.wait_ge(lin_done, 12 + 12 * g + 12)
                        dve.tensor_tensor(v_tok[:, 0:2, :], o_ps[:, 4, :].rearrange("p (t c) -> p t c", t=2),
                                          bv_row[:, None, :].to_broadcast([P, 2, C]), ALU.add).then_inc(v_rows_taken, 1)
                        dve.tensor_tensor(v_tok[:, 2, :], o_ps[:, 5, 0:C], bv_row[:, :], ALU.add)\
                            .then_inc(v_rows_taken, 1)
                        dve.wait_ge(v_rows_taken, 4 * g + 8)
                        dve.sem_inc(v_tok_ok, 1)
                        for n in range(2):
                            dve.wait_ge(hi_ok, 2 * g + n + 1)
                            dve.tensor_tensor(lo[n][par][:, :, :], turned[n][:, :, :], hi[n][par][:, :, :],
                                              ALU.subtract).then_inc(parts_ok, 1)
                        dve.wait_ge(parts_ok, 2 * g + 2)
                        dve.wait_ge(v_hi_ok, g + 1)
                        for t in range(TG):
                            step(dve.scalar_tensor_tensor(
                                out=v_stack[par][:, t, :, HD:2 * HD],
                                in0=v_tok[:, t, :].rearrange("p (h d) -> p h d", d=HD), scalar=V_SCALE,
                                in1=v_stack[par][:, t, :, 0:HD], op0=ALU.mult, op1=ALU.subtract))
                        dve.sem_inc(v_ok, 1)


def attend(nc, a, scr):
    UC = 9
    KC = N // 3
    EXP_LAG, TURN_LAG, AV_LAG = 3, 12, 3
    SPI = B * UC
    JPU, JPI = JM, B * JM
    ITER = NH * GI
    T_RING, PART_RING = 3, 6

    ctx = ExitStack()
    with ctx:
        s = Space(nc, ctx, "att")
        q_sb = [s.sb(f"q{b}", [P, GT], F16) for b in range(B)]
        k_sb = [s.sb(f"k{b}", [P, N], F16) for b in range(B)]
        v_sb = [s.sb(f"v{b}", [P, JM, VS], F16) for b in range(B)]
        mask = [s.sb(f"mask{t}", [P, N]) for t in range(TG)]
        prob = [s.sb(f"prob{i}", [P, TG, N]) for i in range(2)]
        row_max = [s.sb(f"row_max{i}", [P, TG, 3]) for i in range(2)]
        neg_max = [s.sb(f"neg_max{i}", [P, TG]) for i in range(2)]
        shift = s.sb("shift", [P, 3])
        junk = s.sb("junk", [P, 3])
        hi = [s.sb(f"hi{i}", [P, GT], F16) for i in range(PART_RING)]
        lo = [s.sb(f"lo{i}", [P, GT], F16) for i in range(PART_RING)]
        out_sb = [s.sb(f"out{i}", [VS, GT]) for i in range(2)]
        ident = s.sb("ident", [P, P])
        score_ps = [s.ps(f"score{i}", [P, 1024]) for i in range(2)]
        turn_ps = [s.ps(f"turn{i}", [P, 512]) for i in range(T_RING)]
        out_ps = s.ps("out_ps", [P, 512])

        ident_ok = s.sem("ident_ok")
        q_in = [s.sem(f"q_in{b}") for b in range(B)]
        k_in = [s.sem(f"k_in{b}") for b in range(B)]
        v_in = [s.sem(f"v_in{b}") for b in range(B)]
        mask_in = [s.sem(f"mask_in{t}") for t in range(TG)]
        score_done = s.sem("score_done")
        score_taken = s.sem("score_taken")
        max_ok = s.sem("max_ok")
        exp_ok = s.sem("exp_ok")
        turn_done = s.sem("turn_done")
        hi_ok = s.sem("hi_ok")
        lo_ok = s.sem("lo_ok")
        av_done = s.sem("av_done")
        evac_ok = s.sem("evac_ok")
        stored = [s.sem(f"stored{i}") for i in range(2)]
        shift_ok = s.sem("shift_ok")
        passed = s.sem("passed")

        block = ctx.enter_context(nc.Block())

        def loads(sp, h, g, new_head, first):
            it = h * GI + g
            for b in range(B):
                if b == 3:
                    for t in range(TG):
                        if not first:
                            sp.wait_ge(score_taken, 2 + SPI * it - UC + 3 * t + 3)
                        sp.dma_start(mask[t][:, :], a["mask"].rearrange("h (g t p) m -> h g t p m", t=TG, p=P)[h, g, t])\
                            .then_inc(mask_in[t], 16)
                if not first:
                    sp.wait_ge(score_done, SPI * it - SPI + UC * b + UC)
                sp.dma_start(q_sb[b][:, :], scr["q_parts"][h, :, bass.ds(g * GT + b * N, GT)]).then_inc(q_in[b], 16)
                if new_head:
                    sp.dma_start(k_sb[b][:, :], scr["k_parts"][h, :, b * N:(b + 1) * N]).then_inc(k_in[b], 16)
            if new_head:
                for b in range(B):
                    if not first:
                        sp.wait_ge(av_done, PART_RING + JPI * it - JPI + JPU * (b + 1))
                    sp.dma_start(v_sb[b][:, :, :], scr["v_stack"][b, h].rearrange("p (j v) -> p j v", v=VS))\
                        .then_inc(v_in[b], 16)

        @block.sync
        def _(sp):
            loads(sp, 0, 0, True, True)
            with sp.Fori(1, GI) as g:
                loads(sp, 0, g, False, False)
            with sp.Fori(1, NH) as h:
                loads(sp, h, 0, True, False)
                with sp.Fori(1, GI) as g:
                    loads(sp, h, g, False, False)

        @block.gpsimd
        def _(pool):
            make_identity(pool, ident, ident_ok)
            with pool.Fori(0, NH) as h:
                with pool.Fori(0, GI) as g:
                    for b in range(B):
                        u = (h * GI + g) * B + b
                        pool.wait_ge(evac_ok, u + 1)
                        dst = scr["att"].rearrange("k (h d) n -> h k d n", d=HD)
                        for k in range(2):
                            pool.dma_start(dst[h, k, :, bass.ds(g * GT + b * N, GT)],
                                           out_sb[b % 2][k * HD:(k + 1) * HD, :]).then_inc(stored[b % 2], 16)
                        pool.dma_start(scr["att_sum"][bass.ds(h, 1), bass.ds(g * GT + b * N, GT)],
                                       out_sb[b % 2][2 * HD:2 * HD + 1, :]).then_inc(stored[b % 2], 16)
            for i in range(2):
                pool.wait_ge(stored[i], 48 * ITER * B // 2)

        def pe_steps(pe, h, g, new_head, it, ks):
            static = isinstance(it, int)
            for k in ks:
                b, c = k // UC, k % UC
                if not (static and it >= ITER):
                    t, part = c // 3, c % 3
                    if c == 0:
                        pe.wait_ge(q_in[b], it * 16 + 16)
                        pe.wait_ge(k_in[b], h * 16 + 16)
                    pe.wait_ge(score_taken, it * SPI + k + 1)
                    for c0, n in ((0, 512), (512, KC - 512)):
                        last = pe.matmul(score_ps[k % 2][:, c0:c0 + n], q_sb[b][:, t * P:(t + 1) * P],
                                         k_sb[b][:, part * KC + c0:part * KC + c0 + n], start=True, stop=True)
                    last.then_inc(score_done, 1)
                for jj in range(2):
                    j = 2 * (k - TURN_LAG) + jj
                    if not (static and not 0 <= it * JPI + j < ITER * JPI):
                        tb, tj = j // JPU % B, j % JPU
                        if tj == 0:
                            pe.wait_ge(exp_ok, it * SPI + (j // JPU) * UC + UC)
                        pe.wait_ge(lo_ok, it * JPI + j + 1)
                        for t in range(TG):
                            last = pe.transpose(turn_ps[tj % T_RING][:, t * P:(t + 1) * P],
                                                prob[tb % 2][:, t, tj * P:(tj + 1) * P], ident[:, :])
                        last.then_inc(turn_done, 1)
                    j -= AV_LAG
                    if not (static and not 0 <= it * JPI + j < ITER * JPI):
                        ab, aj = j // JPU % B, j % JPU
                        if aj == 0:
                            pe.wait_ge(v_in[ab], h * 16 + (0 if new_head and j < 0 else 16))
                            pe.wait_ge(evac_ok, it * B + j // JPU)
                        pe.wait_ge(lo_ok, T_RING + it * JPI + j + 1)
                        for part in (hi, lo):
                            last = pe.matmul(out_ps[:VS, :GT], v_sb[ab][:, aj, :], part[aj % PART_RING][:, :],
                                             start=(aj == 0 and part is hi), stop=(aj == JPU - 1 and part is lo))
                        last.then_inc(av_done, 1)

        DRAIN = range(0, TURN_LAG + 2)

        @block.tensor
        def _(pe):
            pe.sem_inc(turn_done, 2 * JPU)
            pe.sem_inc(av_done, PART_RING)
            pe.wait_ge(ident_ok, 2)
            pe_steps(pe, 0, 0, True, 0, range(SPI))
            with pe.Fori(1, GI) as g:
                pe_steps(pe, 0, g, False, g, range(SPI))
            with pe.Fori(1, NH) as h:
                pe_steps(pe, h, 0, True, h * GI, range(SPI))
                with pe.Fori(1, GI) as g:
                    pe_steps(pe, h, g, False, h * GI + g, range(SPI))
            pe_steps(pe, NH, 0, True, ITER, DRAIN)

        def act_steps(act, it, ks):
            static = isinstance(it, int)
            for k in ks:
                e = k - EXP_LAG
                if not (static and not 0 <= it * SPI + e < ITER * SPI):
                    b, c = e // UC % B, e % UC
                    t, part = c // 3, c % 3
                    if part == 0:
                        act.wait_ge(max_ok, it * B * TG + e // 3 + 1)
                    span = prob[b % 2][:, t, part * KC:(part + 1) * KC]
                    act.activation(span, span, ACT.Exp, bias=neg_max[b % 2][:, t:t + 1]).then_inc(exp_ok, 1)
                for jj in range(2):
                    j = 2 * (k - TURN_LAG) + jj
                    if not (static and not 0 <= it * JPI + j < ITER * JPI + AV_LAG):
                        tj = j % JPU
                        if not (static and not 0 <= it * JPI + j < ITER * JPI):
                            act.wait_ge(turn_done, 2 * JPU + it * JPI + j + 1)
                            act.wait_ge(av_done, it * JPI + j + 1)
                            act.activation(hi[tj % PART_RING][:, :], turn_ps[tj % T_RING][:, :GT], ACT.Identity)\
                                .then_inc(hi_ok, 1)
                        if tj == AV_LAG - 1 and not (static and it * JPI + j < JPU):
                            u = j // JPU - 1
                            ub = u % B
                            act.wait_ge(av_done, PART_RING + it * JPI + (u + 1) * JPU)
                            act.wait_ge(stored[ub % 2], 48 * (it * 2 + u // 2))
                            act.activation(out_sb[ub % 2][:, :], out_ps[:VS, :GT], ACT.Identity).then_inc(evac_ok, 1)

        @block.scalar
        def _(act):
            act_steps(act, 0, range(SPI))
            with act.Fori(1, ITER) as it:
                act_steps(act, it, range(SPI))
            act_steps(act, ITER, DRAIN)

        def dve_steps(dve, it, ks):
            static = isinstance(it, int)
            for k in ks:
                b, c = k // UC, k % UC
                if not (static and it >= ITER):
                    t, part = c // 3, c % 3
                    if b == 0 and part == 0:
                        dve.wait_ge(mask_in[t], it * 16 + 16)
                    dve.wait_ge(score_done, it * SPI + k + 1)
                    dve.wait_ge(turn_done, it * JPI + b * JPU + (part + 1) * JPU // 3)
                    part_wait(dve, passed)
                    dve.tensor_tensor_reduce(out=prob[b % 2][:, t, part * KC:(part + 1) * KC],
                                             in0=score_ps[k % 2][:, :KC], in1=mask[t][:, part * KC:(part + 1) * KC],
                                             scale=1.0, scalar=-3e38, op0=ALU.add, op1=ALU.max,
                                             accum_out=row_max[b % 2][:, t, part:part + 1]).then_inc(score_taken, 1)
                    if part == 2:
                        dve.wait_ge(score_taken, 2 + it * SPI + k + 1)
                        part_wait(dve, passed)
                        dve.tensor_tensor_reduce(out=junk[:, :], in0=row_max[b % 2][:, t, :], in1=shift[:, :],
                                                 scale=-1.0, scalar=3e38, op0=ALU.add, op1=ALU.min,
                                                 accum_out=neg_max[b % 2][:, t:t + 1]).then_inc(max_ok, 1)
                for jj in range(2):
                    j = 2 * (k - TURN_LAG) + jj
                    if not (static and not 0 <= it * JPI + j < ITER * JPI):
                        tj = j % JPU
                        dve.wait_ge(hi_ok, it * JPI + j + 1)
                        dve.tensor_tensor(lo[tj % PART_RING][:, :], turn_ps[tj % T_RING][:, :GT],
                                          hi[tj % PART_RING][:, :], ALU.subtract).then_inc(lo_ok, 1)

        @block.vector
        def _(dve):
            dve.sem_inc(score_taken, 2)
            dve.sem_inc(lo_ok, T_RING)
            dve.memset(shift[:, :], -P_SHIFT).then_inc(shift_ok, 1)
            dve.wait_ge(shift_ok, 1)
            dve_steps(dve, 0, range(SPI))
            with dve.Fori(1, ITER) as it:
                dve_steps(dve, it, range(SPI))
            dve_steps(dve, ITER, DRAIN)


def mix_and_normalise(nc, a, scr):
    TAPS = 25
    PE_TAPS = list(range(13, TAPS))
    DVE_TAPS = list(range(13))
    WIN = (GR + 4) * PW
    NP = len(PE_TAPS)
    ctx = ExitStack()
    with ctx:
        s = Space(nc, ctx, "mix")
        att = [s.sb(f"att{i}", [P, 3, CC, GT]) for i in range(2)]
        denom = s.sb("denom", [P, NH * M // P])
        win = [s.sb(f"win{i}", [P, CC, WIN]) for i in range(2)]
        x_res = [s.sb(f"x_res{i}", [P, TG, C]) for i in range(2)]
        acc = s.sb("acc", [P, CC, GT])
        yT = [s.sb(f"yT{i}", [P, CC, GT]) for i in range(2)]
        x2 = [s.sb(f"x2{i}", [P, TG, C]) for i in range(2)]
        x_norm = s.sb("x_norm", [P, TG, C])
        tT = [s.sb(f"tT{i}", [P, CC, GT]) for i in range(2)]
        node = [s.sb(f"node{i}", [P, TG, HF + 2 * GHD]) for i in range(2)]
        prod = s.sb("prod", [P, 2, TG, HF])
        stats = s.sb("stats", [P, TG, 6])
        mean_var = s.sb("mean_var", [P, TG, 2])
        rstd = s.sb("rstd", [P, TG])
        newton = s.sb("newton", [P, TG])
        eps = s.sb("eps", [P, 1])
        ident = s.sb("ident", [P, P])
        diag = s.sb("diag", [P, CC, NP, P])
        taps = s.sb("taps", [P, CC, TAPS])
        dw_b = s.sb("dw_b", [P, CC])
        wo = s.sb("wo", [P, CC, C])
        bo_row = s.sb("bo_row", [P, C])
        w_gat = s.sb("w_gat", [P, CC, HF])
        att_rows = s.sb("att_rows", [P, 2, HF])
        conv_ps = [s.ps(f"conv{m}", [P, 512]) for m in range(CC)]
        o_ps = s.ps("o_ps", [P, 4, C])
        t_ps = s.ps("t_ps", [P, CC, 512])
        h_ps = s.ps("h_ps", [P, TG, HF])

        ident_ok = s.sem("ident_ok")
        const_in = s.sem("const_in")
        const_ok = s.sem("const_ok")
        in_ready = [s.sem(f"in_ready{i}") for i in range(2)]
        in_free = s.sem("in_free")
        denom_in = s.sem("denom_in")
        denom_ok = s.sem("denom_ok")
        x_ready = s.sem("x_ready")
        x_free = s.sem("x_free")
        x_res_ok = s.sem("x_res_ok")
        conv_done = s.sem("conv_done")
        yT_ok = s.sem("yT_ok")
        o_done = s.sem("o_done")
        x2_ok = s.sem("x2_ok")
        stats_ok = s.sem("stats_ok")
        root_ok = s.sem("root_ok")
        norm_ok = s.sem("norm_ok")
        turn_done = s.sem("turn_done")
        tT_ok = s.sem("tT_ok")
        h_done = s.sem("h_done")
        node_ok = s.sem("node_ok")
        stored = [s.sem(f"stored{i}") for i in range(2)]
        dve_s = s.sem("dve_s")
        passed = s.sem("passed")

        NCONST = 8
        x_v = a["x"].rearrange("(g t p) c -> g p t c", t=TG, p=P)
        x2_v = scr["x2"].rearrange("(g t p) c -> g p t c", t=TG, p=P)
        node_v = scr["nodes"].rearrange("(g t p) f -> g p t f", t=TG, p=P)
        tT_v = scr["tT"].rearrange("(m p) n -> p m n", p=P)

        block = ctx.enter_context(nc.Block())

        @block.sync
        def _(sp):
            sp.dma_start(taps[:, :, :], a["dw_w"]).then_inc(const_in, 16)
            sp.dma_start(dw_b[:, :], a["dw_b"]).then_inc(const_in, 16)
            sp.dma_start(wo[:, :, :], a["Wo"].rearrange("(k p) n -> p k n", p=P)).then_inc(const_in, 16)
            sp.dma_start(bo_row[:, :], a["bo_row"].to_broadcast([P, C])).then_inc(const_in, 16)
            sp.dma_start(w_gat[:, :, :], a["W_gat"].rearrange("(k p) n -> p k n", p=P)).then_inc(const_in, 16)
            sp.dma_start(att_rows[:, 0, :], a["att_src"].to_broadcast([P, HF])).then_inc(const_in, 16)
            sp.dma_start(att_rows[:, 1, :], a["att_dst"].to_broadcast([P, HF])).then_inc(const_in, 16)
            sp.dma_start(eps[:, :], a["ln_eps"].to_broadcast([P, 1])).then_inc(const_in, 16)

            sp.dma_start(denom[:, :], scr["att_sum"].rearrange("h (q n) -> (h q) n", q=P // NH)).then_inc(denom_in, 16)
            sp.wait_ge(denom_ok, 1)
            sp.dma_start(scr["denom"].rearrange("h (q n) -> (h q) n", q=P // NH), denom[:, :]).then_inc(denom_in, 16)
            sp.wait_ge(denom_in, 32)

            def load(b, gi, g, par):
                for k in range(2):
                    sp.dma_start(att[par][:, k, :, :],
                                 scr["att"].rearrange("k (m p) n -> k p m n", p=P)[k, :, :, bass.ds(g * GT, GT)])\
                        .then_inc(in_ready[par], 16)
                for m in range(CC):
                    sp.dma_start(att[par][:, 2, m, :],
                                 scr["denom"].rearrange("(m h) n -> m h n", m=CC)[m, :, None, bass.ds(g * GT, GT)]
                                 .to_broadcast([P // HD, HD, GT])).then_inc(in_ready[par], 16)
                sp.dma_start(win[par][:, :, :],
                             scr["v_pad"].rearrange("(m p) b n -> b p m n", p=P)[b, :, :, bass.ds(gi * (GR * PW), WIN)])\
                    .then_inc(in_ready[par], 16)

            with sp.Fori(0, B) as b:
                with sp.Fori(0, GI // 2) as gp:
                    for par in range(2):
                        sp.wait_ge(in_free, b * GI + gp * 2 + par + 1)
                        load(b, gp * 2 + par, b * GI + gp * 2 + par, par)
            sp.wait_ge(in_free, NG + 1)
            load(0, 0, 0, 0)

        @block.gpsimd
        def _(pool):
            make_identity(pool, ident, ident_ok)
            pool.wait_ge(const_in, 16 * NCONST)
            with pool.Fori(0, NG // 2) as i:
                for par in range(2):
                    g = 2 * i + par
                    pool.wait_ge(x_free, g + 1)
                    pool.dma_start(x_res[par][:, :, :], x_v[g]).then_inc(x_ready, 16)
                    pool.wait_ge(x_ready, 16 * g + 16)
                    pool.tensor_tensor(x_res[par][:, :, :], x_res[par][:, :, :],
                                       bo_row[:, None, :].to_broadcast([P, TG, C]), ALU.add).then_inc(x_res_ok, 1)

        def pairs(eng, step, last):
            for par in range(2):
                step(par, 0, par, par == 0)
            with eng.Fori(1, NG // 2) as i:
                for par in range(2):
                    step(2 * i + par, i, par, False)
            last()

        @block.scalar
        def _(act):
            def turn(g, i, par):
                act.wait_ge(turn_done, g + 1)
                for m in range(CC):
                    act.activation(tT[par][:, m, :], t_ps[:, m, :GT], ACT.Identity).then_inc(tT_ok, 1)
                act.wait_ge(tT_ok, 2 * g + 2)
                act.dma_start(tT_v[:, :, bass.ds(g * GT, GT)], tT[par][:, :, :]).then_inc(stored[par], 16)
                act.wait_ge(node_ok, g + 1)
                act.dma_start(node_v[g], node[par][:, :, :]).then_inc(stored[par], 16)

            def one(g, i, par, first):
                act.wait_ge(x2_ok, g + 1)
                act.dma_start(x2_v[g], x2[par][:, :, :]).then_inc(stored[par], 16)
                if not first:
                    turn(g - 1, i, 1 - par)
                act.wait_ge(stats_ok, g + 1)
                act.activation(rstd[:, :], mean_var[:, :, 1], ACT.Sqrt, bias=eps[:, :]).then_inc(root_ok, 1)

            pairs(act, one, lambda: turn(NG - 1, NG // 2 - 1, 1))
            for par in range(2):
                act.wait_ge(stored[par], 48 * NG // 2)

        @block.tensor
        def _(pe):
            def conv(g, i, par):
                pe.wait_ge(in_ready[par], 80 * i + 80)
                for m in range(CC):
                    view = win[par][:, m, :].rearrange("p (r w) -> p r w", w=PW)
                    for n, q in enumerate(PE_TAPS):
                        last = pe.matmul(conv_ps[m][:, :GT], diag[:, m, n, :],
                                         view[:, q // 5:q // 5 + GR, q % 5:q % 5 + W],
                                         start=(n == 0), stop=(n == NP - 1))
                last.then_inc(conv_done, 1)

            def turn(g, par):
                pe.wait_ge(norm_ok, g + 1)
                for t in range(TG):
                    for m in range(CC):
                        last = pe.transpose(t_ps[:, m, t * P:(t + 1) * P], x_norm[:, t, m * P:(m + 1) * P], ident[:, :])
                last.then_inc(turn_done, 1)
                pe.wait_ge(tT_ok, 2 * g + 2)
                for t in range(TG):
                    for k in range(CC):
                        last = pe.matmul(h_ps[:, t, :], tT[par][:, k, t * P:(t + 1) * P], w_gat[:, k, :],
                                         start=(k == 0), stop=(k == CC - 1))
                last.then_inc(h_done, 1)

            def one(g, i, par, first):
                pe.wait_ge(yT_ok, 2 * g + 2)
                if not first:
                    pe.wait_ge(x2_ok, g)
                for t in range(TG):
                    for k in range(CC):
                        last = pe.matmul(o_ps[:, t, :], yT[par][:, k, t * P:(t + 1) * P], wo[:, k, :],
                                         start=(k == 0), stop=(k == CC - 1))
                last.then_inc(o_done, 1)
                if not first:
                    turn(g - 1, 1 - par)
                conv(g + 1, i + par, 1 - par)

            pe.wait_ge(const_ok, 1)
            pe.wait_ge(const_in, 16 * NCONST)
            conv(0, 0, 0)
            pairs(pe, one, lambda: turn(NG - 1, 1))

        @block.vector
        def _(dve):
            step = Steps(dve, dve_s)
            dve.sem_inc(in_free, 2)
            dve.sem_inc(x_free, 2)
            dve.wait_ge(denom_in, 16)
            step(dve.reciprocal(denom[:, :], denom[:, :]))
            dve.sem_inc(denom_ok, 1)
            dve.wait_ge(const_in, 16 * NCONST)
            dve.wait_ge(ident_ok, 2)
            for m in range(CC):
                for n, q in enumerate(PE_TAPS):
                    last = dve.tensor_scalar(diag[:, m, n, :], ident[:, :], taps[:, m, q:q + 1], None, ALU.mult)
            last.then_inc(const_ok, 1)

            def mix(g, i, par):
                dve.wait_ge(in_ready[par], 80 * i + 80)
                step(dve.tensor_tensor(att[par][:, 0, :, :], att[par][:, 0, :, :], att[par][:, 1, :, :], ALU.add))
                step(dve.scalar_tensor_tensor(out=acc[:, :, :], in0=att[par][:, 0, :, :], scalar=1.0 / V_SCALE,
                                              in1=att[par][:, 2, :, :], op0=ALU.mult, op1=ALU.mult))
                for q in DVE_TAPS:
                    for m in range(CC):
                        view = win[par][:, m, :].rearrange("p (r w) -> p r w", w=PW)
                        sums = acc[:, m, :].rearrange("p (r w) -> p r w", w=W)
                        step(dve.scalar_tensor_tensor(out=sums, in0=view[:, q // 5:q // 5 + GR, q % 5:q % 5 + W],
                                                      scalar=taps[:, m, q:q + 1], in1=sums,
                                                      op0=ALU.mult, op1=ALU.add), lag=1)
                step.wait()
                dve.wait_ge(conv_done, g + 1)
                for m in range(CC):
                    dve.scalar_tensor_tensor(out=yT[par][:, m, :], in0=conv_ps[m][:, :GT], scalar=dw_b[:, m:m + 1],
                                             in1=acc[:, m, :], op0=ALU.add, op1=ALU.add).then_inc(yT_ok, 1)
                dve.wait_ge(yT_ok, 2 * g + 2)
                dve.sem_inc(in_free, 1)

            def features(g, par):
                dve.wait_ge(h_done, g + 1)
                dve.tensor_copy(node[par][:, :, 0:HF], h_ps[:, :, :])
                for k in range(2):
                    step(dve.tensor_tensor(prod[:, k, :, :], h_ps[:, :, :],
                                           att_rows[:, k, None, :].to_broadcast([P, TG, HF]), ALU.mult))
                for k in range(2):
                    last = dve.tensor_reduce(node[par][:, :, HF + k * GHD:HF + (k + 1) * GHD],
                                             prod[:, k, :, :].rearrange("p t (h x) -> p t h x", x=NX), AX.X, ALU.add)
                last.then_inc(node_ok, 1)

            mix(0, 0, 0)
            MIX = step.n
            FEATURES = 2
            PER = (MIX - 1) + 2 * TG + 5 + FEATURES

            def one(g, i, par, first):
                step.start, step.n = MIX + g * PER - (0 if first else FEATURES), 0
                dve.wait_ge(o_done, g + 1)
                dve.wait_ge(x_res_ok, g + 1)
                if not (isinstance(i, int) and i == 0):
                    dve.wait_ge(stored[par], 48 * i)
                dve.tensor_tensor(x2[par][:, :, :], o_ps[:, 0:TG, :], x_res[par][:, :, :], ALU.add).then_inc(x2_ok, 1)
                dve.wait_ge(x2_ok, g + 1)
                dve.sem_inc(x_free, 1)
                layernorm_stats(dve, step, x2[par], stats, mean_var, TG, passed)
                dve.sem_inc(stats_ok, 1)
                if not first:
                    features(g - 1, 1 - par)
                mix(g + 1, i + par, 1 - par)
                dve.wait_ge(root_ok, g + 1)
                reciprocal_root(dve, step, rstd, mean_var[:, :, 1], newton, LN_EPS)
                for t in range(TG):
                    last = dve.tensor_scalar(x_norm[:, t, :], x2[par][:, t, :], mean_var[:, t, 0:1],
                                             rstd[:, t:t + 1], ALU.subtract, ALU.mult)
                last.then_inc(norm_ok, 1)
                assert step.n == PER - (FEATURES if first else 0)

            def close():
                step.start, step.n = MIX + NG * PER - FEATURES, 0
                features(NG - 1, 1)

            pairs(dve, one, close)


SRC_BITS = 14
PAIR = 2 * ET
OUTER = 16
INNER = EC // PAIR // OUTER


def pack_edges(nc, a, scr):
    ctx = ExitStack()
    with ctx:
        s = Space(nc, ctx, "pack")
        key = s.sb("key", [P, EC], I32)
        src = s.sb("src", [P, EC], I32)
        way = [src, s.sb("way1", [P, EC], I32)]
        dropped = s.sb("dropped", [P, EC])
        before = s.sb("before", [P, EC])
        moves = before[:, :].bitcast(I32)
        kept = s.sb("kept", [P, 1])
        most = s.sb("most", [P, 1])
        count = s.sb("count", [P, 2], I32)
        tail = s.sb("tail", [P, PAIR], I32)
        edge_in = s.sem("edge_in")
        dve_s = s.sem("dve_s")
        passed = s.sem("passed")
        kept_ok = s.sem("kept_ok")
        most_ok = s.sem("most_ok")
        packed = s.sem("packed")
        stored = s.sem("stored")
        block = ctx.enter_context(nc.Block())

        @block.sync
        def _(sp):
            sp.dma_start(src[:, :], a["edges"][0].rearrange("(p e) -> p e", p=P)).then_inc(edge_in, 16)
            sp.dma_start(key[:, :], a["edges"][1].rearrange("(p e) -> p e", p=P)).then_inc(edge_in, 16)
            sp.wait_ge(packed, 1)
            sp.dma_start(scr["keys"][:, 0:EC], key[:, :]).then_inc(stored, 16)
            sp.dma_start(scr["keys"][:, EC:EC + PAIR], tail[:, :]).then_inc(stored, 16)
            sp.dma_start(scr["counts"], count[:, :]).then_inc(stored, 16)
            sp.wait_ge(stored, 48)

        @block.gpsimd
        def _(pool):
            pool.wait_ge(kept_ok, 1)
            pool.partition_all_reduce(most[:, :], kept[:, :], P, REDUCE_MAX)\
                .then_inc(most_ok, 1)

        @block.vector
        def _(dve):
            step = Steps(dve, dve_s)
            dve.wait_ge(edge_in, 32)
            step(dve.tensor_scalar(dropped[:, :], key[:, :], float(M), None, ALU.is_ge))
            step(dve.tensor_tensor_scan(before[:, :], dropped[:, :], dropped[:, :], 0.0, ALU.add, ALU.max))
            step(dve.tensor_scalar(src[:, :], src[:, :], float(M - 1), None, ALU.min))
            step(dve.tensor_scalar(key[:, :], key[:, :], SRC_BITS, None, ALU.logical_shift_left))
            step(dve.tensor_tensor(key[:, :], key[:, :], src[:, :], ALU.bitwise_or))
            dve.tensor_scalar(kept[:, :], before[:, EC - 1:EC], -1.0, float(EC), ALU.mult, ALU.add).then_inc(kept_ok, 1)
            step(dve.scalar_tensor_tensor(out=way[0][:, :], in0=dropped[:, :], scalar=0.0, in1=before[:, :],
                                          op0=ALU.is_equal, op1=ALU.mult))
            for bit in range(EC.bit_length() - 1):
                d = 1 << bit
                old, new = way[bit % 2], way[(bit + 1) % 2]
                step(dve.tensor_scalar(moves, old[:, :], d, None, ALU.bitwise_and))
                step(dve.scalar_tensor_tensor(out=new[:, :], in0=moves, scalar=0.0, in1=old[:, :],
                                              op0=ALU.is_equal, op1=ALU.mult))
                step(dve.copy_predicated(new[:, 0:EC - d], moves[:, d:EC], old[:, d:EC]))
                step(dve.copy_predicated(key[:, 0:EC - d], moves[:, d:EC], key[:, d:EC]))
            step(dve.memset(tail[:, :], 0))
            dve.wait_ge(most_ok, 1)
            step(dve.tensor_copy(count[:, 0:1], most[:, :]))
            dve.tensor_copy(count[:, 1:2], kept[:, :]).then_inc(packed, 1)


def aggregate(nc, a, scr):
    B_RING = 4
    AROWS = LO * TR
    NF = HF + 2 * GHD
    DT = 2 * GHD
    BLK = HI // P
    ctx = ExitStack()
    with ctx:
        s = Space(nc, ctx, "gat")
        nodes = s.sb("nodes", [P, NTILE, NF])
        dst_rows = s.sb("dst_rows", [P, NTILE, DT])
        work = [s.sb(f"work{i}", [P, NTILE, HF]) for i in range(2)]
        loops = s.sb("loops", [P, NTILE, TR])
        sums = s.sb("sums", [P, NTILE, TR])
        peak = s.sb("peak", [P, GHD])
        keys = [s.sb(f"keys{i}", [P, ET], I32) for i in range(2)]
        src_i = [s.sb(f"src_i{i}", [P, ET], I32) for i in range(2)]
        dst_i = [s.sb(f"dst_i{i}", [P, ET], I32) for i in range(2)]
        inside = s.sb("inside", [P, ET])
        left = s.sb("left", [P, 1])
        counts = s.sb("counts", [P, 2], I32)
        lo = [s.sb(f"lo{i}", [P, ET]) for i in range(2)]
        hi = [s.sb(f"hi{i}", [P, ET]) for i in range(2)]
        g_src = [s.sb(f"g_src{i}", [P, ET, NF]) for i in range(2)]
        g_dst = [s.sb(f"g_dst{i}", [P, ET, DT]) for i in range(2)]
        logit = s.sb("logit", [P, ET, GHD])
        logit2 = s.sb("logit2", [P, ET, GHD])
        val = s.sb("val", [P, ET, TR])
        rest = s.sb("rest", [P, ET, TR])
        part = [s.sb(f"part{i}", [P, ET, TR], BF16) for i in range(3)]
        one_lo = s.sb("one_lo", [P, ET, LO], BF16)
        spread = [[s.sb(f"spread{i}{k}", [P, ET, LO, TR], BF16) for k in range(3)] for i in range(2)]
        one_hi = [s.sb(f"one_hi{i}", [P, HI], BF16) for i in range(B_RING)]
        iota_i = s.sb("iota_i", [P, HI], I32)
        iota_hi = s.sb("iota_hi", [P, HI], F16)
        iota_f = s.sb("iota_f", [P, ET])
        zeros = s.sb("zeros", [P, 512], BF16)
        ident = s.sb("ident", [P, P])
        acc_sb = s.sb("acc_sb", [AROWS, HI])
        b_gat = s.sb("b_gat", [P, HF])
        gamma = s.sb("gamma", [P, HF])
        beta = s.sb("beta", [P, HF])
        small = [s.sb(f"small{i}", [P, NTILE]) for i in range(4)]
        score = s.sb("score", [P, NTILE, NX])
        rank = s.sb("rank", [P, NTILE, NX])
        gates = s.sb("gates", [P, NTILE, NX])
        eps = s.sb("eps", [P, 1])
        acc = s.ps("acc", [P, 3, 512])
        t_ps = s.ps("t_ps", [P, 4, 512])

        ident_ok = s.sem("ident_ok")
        const_in = s.sem("const_in")
        dve_s = s.sem("dve_s")
        passed = s.sem("passed")
        peak_ok = s.sem("peak_ok")
        peak_all = s.sem("peak_all")
        table_ok = s.sem("table_ok")
        table_out = s.sem("table_out")
        exp_in = s.sem("exp_in")
        exp_out = s.sem("exp_out")
        keys_in = [s.sem(f"keys_in{i}") for i in range(2)]
        keys_free = s.sem("keys_free")
        decoded = s.sem("decoded")
        index_free = s.sem("index_free")
        src_got = [s.sem(f"src_got{i}") for i in range(2)]
        dst_got = [s.sem(f"dst_got{i}") for i in range(2)]
        logit_ok = s.sem("logit_ok")
        weight_ok = s.sem("weight_ok")
        spread_ok = s.sem("spread_ok")
        one_ok = s.sem("one_ok")
        tile_done = s.sem("tile_done")
        acc_done = s.sem("acc_done")
        evac_ok = s.sem("evac_ok")
        block_turned = s.sem("block_turned")
        block_taken = s.sem("block_taken")
        root_in = s.sem("root_in")
        root_out = s.sem("root_out")
        tail_s = s.sem("tail_s")
        done = s.sem("done")
        stored = s.sem("stored")

        block = ctx.enter_context(nc.Block())

        def edge_loop(eng, body):
            most = eng.value_load(counts[0:1, 0:1], min_val=0, max_val=EC)
            with eng.Fori(0, OUTER) as o:
                with eng.If(o * (INNER * PAIR) < most):
                    with eng.Fori(0, INNER) as n:
                        with eng.If((o * INNER + n) * PAIR < most):
                            body(o * INNER + n)

        @block.sync
        def _(sp):
            sp.dma_start(counts[:, :], scr["counts"]).then_inc(const_in, 16)
            sp.dma_start(nodes[:, :, :], scr["nodes"].rearrange("(t p) f -> p t f", p=P)).then_inc(const_in, 16)
            for dst, n in ((b_gat, "b_gat"), (gamma, "ln_gamma"), (beta, "ln_beta")):
                sp.dma_start(dst[:, :], a[n].to_broadcast([P, HF])).then_inc(const_in, 16)
            sp.dma_start(eps[:, :], a["ln_eps"].to_broadcast([P, 1])).then_inc(const_in, 16)
            sp.wait_ge(table_ok, 1)
            sp.dma_start(scr["dst_table"].rearrange("(t p) f -> p t f", p=P), dst_rows[:, :, :]).then_inc(table_out, 16)
            sp.wait_ge(const_in, 96)
            sp.dma_start(keys[0][:, :], scr["keys"][:, 0:ET]).then_inc(keys_in[0], 16)

            def body(c):
                for par in range(2):
                    sp.wait_ge(keys_free, 2 * c + par + 1)
                    sp.dma_start(keys[1 - par][:, :], scr["keys"][:, bass.ds(c * PAIR + (par + 1) * ET, ET)])\
                        .then_inc(keys_in[1 - par], 16)

            edge_loop(sp, body)
            sp.wait_ge(done, 1)
            sp.dma_start(scr["gates"].rearrange("(t p) f -> p t f", p=P), gates[:, :, :]).then_inc(stored, 16)
            sp.wait_ge(stored, 16)

        @block.gpsimd
        def _(pool):
            make_identity(pool, ident, ident_ok)
            pool.iota(iota_i[:, :], pattern=[[1, HI]], base=0, channel_multiplier=0).then_inc(ident_ok, 1)
            pool.wait_ge(peak_ok, 1)
            pool.partition_all_reduce(peak[:, :], peak[:, :], P, REDUCE_MAX).then_inc(peak_all, 1)
            pool.wait_ge(const_in, 96)
            pool.wait_ge(table_out, 16)

            def body(c):
                for par in range(2):
                    pool.wait_ge(decoded, 2 * c + par + 1)
                    pool.wait_ge(weight_ok, 2 * c + par + 1)
                    part_wait(pool, passed)
                    for t in range(ET):
                        pool.indirect_dma_start(g_src[par][:, t, :], None, scr["nodes"],
                                                bass.IndirectOffsetOnAxis(src_i[par][:, t:t + 1].bitcast(U32), 0))\
                            .then_inc(src_got[par], 16)
                        pool.indirect_dma_start(g_dst[par][:, t, :], None, scr["dst_table"],
                                                bass.IndirectOffsetOnAxis(dst_i[par][:, t:t + 1].bitcast(U32), 0))\
                            .then_inc(dst_got[par], 16)

            edge_loop(pool, body)

        @block.scalar
        def _(act):
            act.wait_ge(exp_in, 1)
            act.activation(loops[:, :, HF:], work[0][:, :, 0:GHD], ACT.Exp).then_inc(exp_out, 1)
            act.wait_ge(const_in, 96)

            def body(c):
                for par in range(2):
                    act.wait_ge(logit_ok, 2 * c + par + 1)
                    act.activation(val[:, :, HF:], logit[:, :, :], ACT.Exp).then_inc(exp_out, 1)

            edge_loop(act, body)
            act.wait_ge(root_in, 1)
            act.activation(small[2][:, :], small[1][:, :], ACT.Sqrt, bias=eps[:, :]).then_inc(root_out, 1)
            act.wait_ge(root_in, 2)
            act.activation(gates[:, :, :], score[:, :, :], ACT.Exp).then_inc(root_out, 1)

        @block.tensor
        def _(pe):
            pe.wait_ge(ident_ok, 2)
            pe.wait_ge(table_ok, 1)
            pe.wait_ge(const_in, 96)
            for n in range(3):
                pe.matmul(acc[:AROWS, n, :], zeros[:, 0:AROWS], zeros[:, :], start=True, stop=False, skip_group_check=True)

            def body(c):
                for par in range(2):
                    pe.wait_ge(spread_ok, 2 * c + par + 1)
                    for t in range(ET):
                        pe.wait_ge(one_ok, (2 * c + par) * ET + t + 1)
                        for k in range(3):
                            for n in range(3):
                                last = pe.matmul(acc[:AROWS, n, :],
                                                 spread[par][k][:, t, :, :].rearrange("p l f -> p (l f)"),
                                                 one_hi[t % B_RING][:, n * 512:(n + 1) * 512],
                                                 start=False, stop=False, skip_group_check=True)
                        last.then_inc(tile_done, 1)

            edge_loop(pe, body)
            for n in range(3):
                last = pe.matmul(acc[:AROWS, n, :], zeros[:, 0:AROWS], zeros[:, :], start=False, stop=True,
                                 skip_group_check=True)
            last.then_inc(acc_done, 1)
            pe.wait_ge(evac_ok, 1)
            for k in range(BLK):
                if k >= 4:
                    pe.wait_ge(block_taken, k - 3)
                pe.transpose(t_ps[:, k % 4, 0:AROWS], acc_sb[:, k * P:(k + 1) * P], ident[:AROWS, :AROWS])\
                    .then_inc(block_turned, 1)

        @block.vector
        def _(dve):
            step = Steps(dve, dve_s)

            def leaky(out, x):
                step(dve.scalar_tensor_tensor(out=out, in0=x, scalar=0.2, in1=x, op0=ALU.mult, op1=ALU.max))

            def over_heads(ap):
                return ap.rearrange("p t (h x) -> p t h x", x=NX)

            dve.wait_ge(const_in, 96)
            dve.wait_ge(ident_ok, 3)
            step(dve.memset(zeros[:, :], 0.0))
            step(dve.tensor_scalar(iota_hi[:, :], iota_i[:, :], 1.0, None, ALU.add))
            step(dve.tensor_copy(iota_f[:, :], iota_i[:, 0:ET]))
            step(dve.tensor_copy(left[:, :], counts[:, 1:2]))
            src_logit = nodes[:, :, HF:HF + GHD]
            dst_logit = nodes[:, :, HF + GHD:NF]
            dve.tensor_reduce(peak[:, :], src_logit.rearrange("p t h -> p h t"), AX.X, ALU.max).then_inc(peak_ok, 1)
            dve.wait_ge(peak_all, 1)
            step(dve.tensor_tensor(work[0][:, :, 0:GHD], dst_logit, peak[:, None, :].to_broadcast([P, NTILE, GHD]), ALU.add))
            leaky(dst_rows[:, :, GHD:], work[0][:, :, 0:GHD])
            step(dve.tensor_copy(dst_rows[:, :, 0:GHD], dst_logit))
            dve.sem_inc(table_ok, 1)
            step(dve.tensor_tensor(work[0][:, :, 0:GHD], src_logit, dst_logit, ALU.add))
            leaky(work[0][:, :, GHD:2 * GHD], work[0][:, :, 0:GHD])
            step(dve.tensor_tensor(work[0][:, :, 0:GHD], work[0][:, :, GHD:2 * GHD], dst_rows[:, :, GHD:], ALU.subtract))
            dve.sem_inc(exp_in, 1)
            dve.wait_ge(exp_out, 1)
            step(dve.tensor_tensor(over_heads(loops[:, :, 0:HF]), over_heads(nodes[:, :, 0:HF]),
                                   loops[:, :, HF:, None].to_broadcast([P, NTILE, GHD, NX]), ALU.mult))

            dve.sem_inc(weight_ok, 2)

            def decode(n, i, par):
                dve.wait_ge(keys_in[par], 16 * i + 16)
                step(dve.tensor_scalar(src_i[par][:, :], keys[par][:, :], (1 << SRC_BITS) - 1, None, ALU.bitwise_and))
                step(dve.tensor_scalar(dst_i[par][:, :], keys[par][:, :], SRC_BITS, None, ALU.logical_shift_right))
                dve.sem_inc(keys_free, 1)
                step(dve.tensor_scalar(inside[:, :], iota_f[:, :], left[:, 0:1], None, ALU.is_lt))
                step(dve.tensor_scalar(left[:, :], left[:, :], float(ET), None, ALU.subtract))
                step(dve.tensor_tensor(src_i[par][:, :], src_i[par][:, :], inside[:, :], ALU.mult))
                step(dve.tensor_tensor(dst_i[par][:, :], dst_i[par][:, :], inside[:, :], ALU.mult))
                dve.sem_inc(decoded, 1)
                step(dve.tensor_scalar(lo[par][:, :], dst_i[par][:, :], float(HI), None, ALU.is_ge))
                for j in range(2, LO):
                    step(dve.scalar_tensor_tensor(out=lo[par][:, :], in0=dst_i[par][:, :], scalar=float(j * HI),
                                                  in1=lo[par][:, :], op0=ALU.is_ge, op1=ALU.add))
                step(dve.scalar_tensor_tensor(out=hi[par][:, :], in0=lo[par][:, :], scalar=-float(HI),
                                              in1=dst_i[par][:, :], op0=ALU.mult, op1=ALU.add))
                step(dve.scalar_tensor_tensor(out=hi[par][:, :], in0=hi[par][:, :], scalar=1.0,
                                              in1=inside[:, :], op0=ALU.add, op1=ALU.mult))

            def process(n, i, par, gathers):
                dve.wait_ge(src_got[par], 16 * gathers * (i + 1))
                dve.wait_ge(dst_got[par], 16 * gathers * (i + 1))
                step(dve.tensor_tensor(logit[:, :, :], g_src[par][:, :, HF:HF + GHD], g_dst[par][:, :, 0:GHD], ALU.add))
                leaky(logit2[:, :, :], logit[:, :, :])
                step(dve.tensor_tensor(logit[:, :, :], logit2[:, :, :], g_dst[par][:, :, GHD:], ALU.subtract))
                dve.sem_inc(logit_ok, 1)
                step(dve.tensor_tensor(one_lo[:, :, :], lo[par][:, :, None].to_broadcast([P, ET, LO]),
                                       iota_f[:, None, 0:LO].to_broadcast([P, ET, LO]), ALU.is_equal))
                dve.wait_ge(exp_out, n + 2)
                step(dve.tensor_tensor(over_heads(val[:, :, 0:HF]), over_heads(g_src[par][:, :, 0:HF]),
                                       val[:, :, HF:, None].to_broadcast([P, ET, GHD, NX]), ALU.mult))
                dve.sem_inc(weight_ok, 1)
                step(dve.tensor_copy(part[0][:, :, :], val[:, :, :]))
                step(dve.tensor_tensor(rest[:, :, :], val[:, :, :], part[0][:, :, :], ALU.subtract))
                step(dve.tensor_copy(part[1][:, :, :], rest[:, :, :]))
                step(dve.tensor_tensor(part[2][:, :, :], rest[:, :, :], part[1][:, :, :], ALU.subtract))
                dve.wait_ge(tile_done, ET * (n + 1))
                for k in range(3):
                    step(dve.tensor_tensor(spread[par][k][:, :, :, :],
                                           one_lo[:, :, :, None].to_broadcast([P, ET, LO, TR]),
                                           part[k][:, :, None, :].to_broadcast([P, ET, LO, TR]), ALU.mult))
                dve.sem_inc(spread_ok, 1)
                for t in range(ET):
                    dve.wait_ge(tile_done, ET * n + t + 2 * ET - B_RING + 1)
                    dve.tensor_scalar(one_hi[t % B_RING][:, :], iota_hi[:, :], hi[par][:, t:t + 1], None, ALU.is_equal)\
                        .then_inc(one_ok, 1)

            dve.sem_inc(tile_done, 2 * ET)
            decode(0, 0, 0)
            before_loop = step.n
            sizes = []

            def body(c):
                start = before_loop + c * PER
                step.start, step.n = start, 0
                for par in range(2):
                    decode(2 * c + par + 1, c + par, 1 - par)
                    process(2 * c + par, c, par, ET)
                sizes.append(step.n)

            PER = 2 * (13 + 12)
            edge_loop(dve, body)
            assert sizes == [PER], sizes
            step = Steps(dve, tail_s)
            dve.wait_ge(acc_done, 1)
            dve.tensor_copy(acc_sb[:, :].rearrange("p (n c) -> p n c", n=3), acc[:AROWS, :, :]).then_inc(evac_ok, 1)
            for k in range(BLK):
                dve.wait_ge(block_turned, k + 1)
                dve.tensor_copy(sums[:, k:NTILE:BLK, :], t_ps[:, k % 4, 0:AROWS].rearrange("p (l f) -> p l f", l=LO))\
                    .then_inc(block_taken, 1)
            dve.wait_ge(block_taken, BLK)
            step(dve.tensor_tensor(sums[:, :, :], sums[:, :, :], loops[:, :, :], ALU.add))
            step(dve.reciprocal(sums[:, :, HF:], sums[:, :, HF:]))
            agg, square = work
            step(dve.tensor_tensor(over_heads(agg[:, :, :]), over_heads(sums[:, :, 0:HF]),
                                   sums[:, :, HF:, None].to_broadcast([P, NTILE, GHD, NX]), ALU.mult))

            def row(ap):
                return ap[:, None, :].to_broadcast([P, NTILE, HF])

            def col(ap, n):
                return ap[:, :, None].to_broadcast([P, NTILE, n])

            step(dve.tensor_tensor(agg[:, :, :], agg[:, :, :], row(b_gat), ALU.add))
            step(dve.tensor_reduce(small[0][:, :], agg[:, :, :], AX.X, ALU.add))
            step(dve.tensor_scalar(small[0][:, :], small[0][:, :], 1.0 / HF, None, ALU.mult))
            step(dve.tensor_tensor(agg[:, :, :], agg[:, :, :], col(small[0], HF), ALU.subtract))
            step(dve.tensor_tensor(square[:, :, :], agg[:, :, :], agg[:, :, :], ALU.mult))
            step(dve.tensor_reduce(small[1][:, :], square[:, :, :], AX.X, ALU.add))
            step(dve.tensor_scalar(small[1][:, :], small[1][:, :], 1.0 / HF, None, ALU.mult))
            dve.sem_inc(root_in, 1)
            dve.wait_ge(root_out, 1)
            reciprocal_root(dve, step, small[2], small[1][:, :], small[3], LN_EPS)
            step(dve.tensor_tensor(agg[:, :, :], agg[:, :, :], col(small[2], HF), ALU.mult))
            step(dve.tensor_tensor(agg[:, :, :], agg[:, :, :], row(gamma), ALU.mult))
            step(dve.tensor_tensor(agg[:, :, :], agg[:, :, :], row(beta), ALU.add))
            step(dve.tensor_reduce(score[:, :, :], agg[:, :, :].rearrange("p t (h x) -> p t x h", x=NX), AX.X, ALU.add))
            step(dve.tensor_scalar(score[:, :, :], score[:, :, :], 1.0 / GHD, None, ALU.mult))
            for i in range(NX):
                step(dve.memset(rank[:, :, i], float(NX - 1 - i)))
            for i in range(NX):
                for j in range(i + 1, NX):
                    step(dve.tensor_tensor(small[0][:, :], score[:, :, i], score[:, :, j], ALU.is_ge))
                    step(dve.tensor_tensor(rank[:, :, j], rank[:, :, j], small[0][:, :], ALU.add))
                    step(dve.tensor_tensor(rank[:, :, i], rank[:, :, i], small[0][:, :], ALU.subtract))
            step(dve.tensor_reduce(small[0][:, :], score[:, :, :], AX.X, ALU.max))
            step(dve.tensor_tensor(score[:, :, :], score[:, :, :], col(small[0], NX), ALU.subtract))
            step(dve.tensor_scalar(rank[:, :, :], rank[:, :, :], 1.5, None, ALU.is_lt))
            dve.sem_inc(root_in, 1)
            dve.wait_ge(root_out, 2)
            step(dve.tensor_tensor(gates[:, :, :], gates[:, :, :], rank[:, :, :], ALU.mult))
            step(dve.tensor_reduce(small[0][:, :], gates[:, :, :], AX.X, ALU.add))
            step(dve.reciprocal(small[0][:, :], small[0][:, :]))
            step(dve.tensor_tensor(gates[:, :, :], gates[:, :, :], col(small[0], NX), ALU.mult))
            dve.sem_inc(done, 1)


def experts(nc, a, scr, out):
    FC = GF // P
    ctx = ExitStack()
    with ctx:
        s = Space(nc, ctx, "ffn")
        tT = [s.sb(f"tT{i}", [P, CC, GT]) for i in range(2)]
        total = [s.sb(f"total{i}", [P, TG, C]) for i in range(2)]
        gates = s.sb("gates", [P, NTILE, NX])
        w1 = s.sb("w1", [P, CC, NX, GF])
        w2 = s.sb("w2", [P, NX, FC, C])
        b1 = s.sb("b1", [P, NX, FC])
        b2_row = s.sb("b2_row", [P, NX, C])
        hidden = [s.sb(f"hidden{i}", [P, FC, GT]) for i in range(2)]
        h_ps = [s.ps(f"h{i}", [P, 512]) for i in range(FC)]
        y_ps = [s.ps(f"y{i}", [P, 4, C]) for i in range(2)]

        const_in = s.sem("const_in")
        t_in = [s.sem(f"t_in{i}") for i in range(2)]
        x_in = [s.sem(f"x_in{i}") for i in range(2)]
        h_done = s.sem("h_done")
        gelu_ok = s.sem("gelu_ok")
        y_done = s.sem("y_done")
        y_taken = s.sem("y_taken")
        total_ok = s.sem("total_ok")
        total_free = s.sem("total_free")
        stored = [s.sem(f"stored{i}") for i in range(2)]
        dve_s = s.sem("dve_s")
        passed = s.sem("passed")

        x2_v = scr["x2"].rearrange("(g t p) c -> g p t c", t=TG, p=P)
        out_v = out.rearrange("(g t p) c -> g p t c", t=TG, p=P)
        tT_v = scr["tT"].rearrange("(m p) n -> p m n", p=P)
        block = ctx.enter_context(nc.Block())

        @block.sync
        def _(sp):
            for k in range(CC):
                sp.dma_start(w1[:, k, :, :], a["W1"].rearrange("x (k p) f -> k p x f", p=P)[k]).then_inc(const_in, 16)
            for x in range(NX):
                sp.dma_start(w2[:, x, :, :], a["W2"][x].rearrange("(k p) c -> p k c", p=P)).then_inc(const_in, 16)
                sp.dma_start(b2_row[:, x, :], a["b2"][x:x + 1, :].to_broadcast([P, C])).then_inc(const_in, 16)
            sp.dma_start(b1[:, :, :], a["b1"]).then_inc(const_in, 16)
            sp.dma_start(gates[:, :, :], scr["gates"].rearrange("(t p) f -> p t f", p=P)).then_inc(const_in, 16)
            with sp.Fori(0, NG // 2) as i:
                for par in range(2):
                    g = 2 * i + par
                    sp.wait_ge(h_done, NX * FC * (g + 1))
                    sp.dma_start(tT[par][:, :, :], tT_v[:, :, bass.ds(g * GT, GT)]).then_inc(t_in[par], 16)
                    sp.wait_ge(total_free, g + 1)
                    sp.dma_start(total[par][:, :, :], x2_v[g]).then_inc(x_in[par], 16)
            sp.wait_ge(h_done, NX * FC * (NG + 1))
            sp.dma_start(tT[0][:, :, :], tT_v[:, :, 0:GT]).then_inc(t_in[0], 16)

        @block.gpsimd
        def _(pool):
            pool.sem_inc(total_free, 2)
            with pool.Fori(0, NG // 2) as i:
                for par in range(2):
                    pool.wait_ge(total_ok, 2 * i + par + 1)
                    pool.dma_start(out_v[2 * i + par], total[par][:, :, :]).then_inc(stored[par], 16)
                    pool.wait_ge(stored[par], 16 * i + 16)
                    pool.sem_inc(total_free, 1)

        @block.scalar
        def _(act):
            act.sem_inc(gelu_ok, FC)
            act.wait_ge(const_in, 16 * (CC + 2 * NX + 2))

            def gelu(u, e):
                act.wait_ge(y_done, u + 1)
                for c in range(FC):
                    act.wait_ge(h_done, 2 * NX * FC + u * FC + c + 1)
                    act.activation(hidden[e % 2][:, c, :], h_ps[c][:, :GT], ACT.Gelu, bias=b1[:, e, c:c + 1])\
                        .then_inc(gelu_ok, 1)

            with act.Fori(0, NG) as g:
                for e in range(NX):
                    gelu(g * NX + e, e)
            gelu(NG * NX, 0)

        @block.tensor
        def _(pe):
            pe.sem_inc(h_done, 2 * NX * FC)
            pe.sem_inc(y_done, 2)
            pe.wait_ge(const_in, 16 * (CC + 2 * NX + 2))

            def hide(g, i, par, e):
                if e == 0:
                    pe.wait_ge(t_in[par], 16 * i + 16)
                for c in range(FC):
                    pe.wait_ge(gelu_ok, (g * NX + e) * FC + c + 1)
                    for k in range(CC):
                        last = pe.matmul(h_ps[c][:, :GT], w1[:, k, e, c * P:(c + 1) * P], tT[par][:, k, :],
                                         start=(k == 0), stop=(k == CC - 1))
                    last.then_inc(h_done, 1)

            hide(0, 0, 0, 0)
            with pe.Fori(0, NG // 2) as i:
                for par in range(2):
                    g = 2 * i + par
                    for e in range(NX):
                        if e < NX - 1:
                            hide(g, i, par, e + 1)
                        else:
                            hide(g + 1, i + par, 1 - par, 0)
                        u = g * NX + e
                        pe.wait_ge(gelu_ok, FC + u * FC + FC)
                        pe.wait_ge(y_taken, u + 1)
                        for t in range(TG):
                            for c in range(FC):
                                last = pe.matmul(y_ps[e % 2][:, t, :], hidden[e % 2][:, c, t * P:(t + 1) * P],
                                                 w2[:, e, c, :], start=(c == 0), stop=(c == FC - 1))
                        last.then_inc(y_done, 1)

        @block.vector
        def _(dve):
            step = Steps(dve, dve_s)
            dve.sem_inc(y_taken, 2)
            dve.wait_ge(const_in, 16 * (CC + 2 * NX + 2))
            PER = 2 * NX * TG
            with dve.Fori(0, NG // 2) as i:
                for par in range(2):
                    g = 2 * i + par
                    step.start, step.n = g * PER, 0
                    dve.wait_ge(x_in[par], 16 * i + 16)
                    for e in range(NX):
                        if e == 0:
                            for x in range(NX):
                                for t in range(TG):
                                    step(dve.scalar_tensor_tensor(
                                        out=total[par][:, t, :], in0=b2_row[:, x, :],
                                        scalar=gates[:, bass.ds(g * TG + t, 1), x], in1=total[par][:, t, :],
                                        op0=ALU.mult, op1=ALU.add), lag=TG - 1)
                        dve.wait_ge(y_done, 2 + g * NX + e + 1)
                        for t in range(TG):
                            step(dve.scalar_tensor_tensor(
                                out=total[par][:, t, :], in0=y_ps[e % 2][:, t, :],
                                scalar=gates[:, bass.ds(g * TG + t, 1), e], in1=total[par][:, t, :],
                                op0=ALU.mult, op1=ALU.add), lag=TG - 1)
                        dve.wait_ge(dve_s, step.start + step.n)
                        dve.sem_inc(y_taken, 1)
                    dve.sem_inc(total_ok, 1)
                    assert step.n == PER


_OUT = (B, H, W, C)


def layouts(i):
    conv = {n: i["L0_conv_" + n] for n in ("sin", "cos", "mask", "Wq", "bq", "Wk", "bk", "Wv", "bv", "dw_w", "dw_b", "Wo", "bo")}
    ffn = {n: i["L0_ffn_" + n] for n in ("W_gat", "att_src", "att_dst", "b_gat", "ln_gamma", "ln_beta", "W1", "b1", "W2", "b2")}
    swap = np.arange(C) ^ 1

    def column(v):
        return v.reshape(CC, P).T

    return {
        "x": i["x"].reshape(M, C),
        "Wq": conv["Wq"], "Wq_swap": conv["Wq"][:, swap], "Wk": conv["Wk"], "Wk_swap": conv["Wk"][:, swap],
        "Wv": conv["Wv"], "Wo": conv["Wo"],
        "bq": column(conv["bq"]), "bq_swap": column(conv["bq"][swap]),
        "bk": column(conv["bk"]), "bk_swap": column(conv["bk"][swap]),
        "bv": column(conv["bv"]), "bv_row": conv["bv"].reshape(1, C), "bo_row": conv["bo"].reshape(1, C),
        "cos": conv["cos"].reshape(N, HD).T, "sin": conv["sin"].reshape(N, HD).T,
        "sign": np.where(np.arange(P) % 2 == 0, -1.0, 1.0).astype(np.float32).reshape(P, 1),
        "ln_eps": np.full((1, 1), LN_EPS, np.float32),
        "mask": conv["mask"],
        "dw_w": conv["dw_w"].reshape(25, CC, P).transpose(2, 1, 0), "dw_b": column(conv["dw_b"]),
        "W_gat": ffn["W_gat"], "att_src": ffn["att_src"].reshape(1, HF), "att_dst": ffn["att_dst"].reshape(1, HF),
        "b_gat": ffn["b_gat"].reshape(1, HF), "ln_gamma": ffn["ln_gamma"].reshape(1, HF),
        "ln_beta": ffn["ln_beta"].reshape(1, HF),
        "W1": ffn["W1"], "b1": ffn["b1"].reshape(NX, GF // P, P).transpose(2, 0, 1), "W2": ffn["W2"], "b2": ffn["b2"],
        "edges": i["L0_ffn_edge_index"],
    }


def metaformer(nc, a, out):
    shapes = {
        "q_parts": ((NH, 4 * HD, M), F16), "k_parts": ((NH, 4 * HD, M), F16),
        "v_stack": ((B, NH, P, JM * VS), F16), "v_pad": ((C, B, PH * PW), F32),
        "att": ((2, C, M), F32), "att_sum": ((NH, M), F32), "denom": ((NH, M), F32), "x2": ((M, C), F32), "tT": ((C, M), F32),
        "nodes": ((M, HF + 2 * GHD), F32), "dst_table": ((M, 2 * GHD), F32),
        "keys": ((P, EC + PAIR), I32), "counts": ((P, 2), I32), "gates": ((M, NX), F32),
    }
    scr = {n: nc.dram_tensor(f"scr_{n}", shape, dt, kind="Internal").ap() for n, (shape, dt) in shapes.items()}
    pack_edges(nc, a, scr)
    project_qkv(nc, a, scr)
    attend(nc, a, scr)
    mix_and_normalise(nc, a, scr)
    aggregate(nc, a, scr)
    experts(nc, a, scr, out)


def kernel(**inputs):
    import concourse.bacc as bacc
    from concourse.bass_utils import run_bass_kernel_spmd

    nc = bacc.Bacc("TRN2", target_bir_lowering=False, num_devices=1)
    arrays, aps = {}, {}
    for name, v in layouts({n: np.asarray(v) for n, v in inputs.items()}).items():
        v = np.ascontiguousarray(v)
        arrays[f"in_{name}"] = v
        aps[name] = nc.dram_tensor(f"in_{name}", v.shape, mybir.dt.from_np(v.dtype), kind="ExternalInput").ap()
    out = nc.dram_tensor("out", (M, C), F32, kind="ExternalOutput").ap()
    metaformer(nc, aps, out)
    r = run_bass_kernel_spmd(nc, [arrays], core_ids=[0])
    return r.results[0]["out"].reshape(_OUT)
```

```python
from contextlib import ExitStack

import numpy as np

import concourse.bass as bass
from concourse import mybir

F32 = mybir.dt.float32
F16 = mybir.dt.float16
BF16 = mybir.dt.bfloat16
I32 = mybir.dt.int32
I16 = mybir.dt.int16
U32 = mybir.dt.uint32
ALU = mybir.AluOpType
ACT = mybir.ActivationFunctionType
AX = mybir.AxisListType
REDUCE_MAX = bass.bass_isa.ReduceOp.max

B, H, W, C = 4, 48, 48, 256
NH, HD = 8, 32
N = H * W
M = B * N
P = 128
CC = C // P
TG = 3
GT = TG * P
GI = N // GT
NG = M // GT
GR = GT // W
PH, PW = H + 4, W + 4
VS = 3 * HD
V_SCALE = 64.0
P_SHIFT = 14 * float(np.log(2.0))
JM = N // P

NX, GF, GHD = 4, 512, 4
HF = GHD * NX
TR = HF + GHD
E = 1048576
EC = E // P
ET = 16
LO, HI = 6, 1536
NTILE = M // P
FC = GF // P
FG = 2
FT = FG * P
NFG = M // FT
LN_EPS = 1e-5
SRC_BITS = 14
PAIR = 2 * ET
OUTER = 20
INNER = (EC // PAIR - NFG) // OUTER


class Steps:

    def __init__(self, eng, sem, start=0):
        self.eng, self.sem, self.start, self.n = eng, sem, start, 0

    def __call__(self, ins, lag=0):
        self.mark(ins)
        if self.n > lag:
            self.eng.wait_ge(self.sem, self.start + self.n - lag)

    def mark(self, ins):
        self.n += 1
        ins.then_inc(self.sem, 1)

    def wait(self):
        self.eng.wait_ge(self.sem, self.start + self.n)


class Space:

    def __init__(self, nc, ctx, tag):
        self.nc, self.ctx, self.tag = nc, ctx, tag

    def sb(self, name, shape, dt=F32):
        return self.ctx.enter_context(self.nc.sbuf_tensor(f"{self.tag}_{name}", shape, dt))

    def ps(self, name, shape, dt=F32):
        return self.ctx.enter_context(self.nc.psum_tensor(f"{self.tag}_{name}", shape, dt))

    def sem(self, name):
        return self.ctx.enter_context(self.nc.semaphore(f"{self.tag}_{name}"))


def make_identity(pool, ident, sem):
    pool.memset(ident[:, :], 0.0).then_inc(sem, 1)
    pool.wait_ge(sem, 1)
    pool.affine_select(out=ident[:, :], in_=ident[:, :], compare_op=ALU.not_equal, fill=1.0,
                       base=0, pattern=[[-1, P]], channel_multiplier=1).then_inc(sem, 1)


def part_wait(eng, passed):
    eng.sem_inc(passed, 1)


def layernorm_stats(dve, step, x_tiles, stats, mean_var, tiles, passed):
    for t in range(tiles):
        step.mark(dve.bn_stats(stats[:, t, :], x_tiles[:, t, :]))
    step.wait()
    part_wait(dve, passed)
    for t in range(tiles):
        step.mark(dve.bn_aggr(mean_var[:, t, :], stats[:, t, :]))
    step.wait()


def reciprocal_root(dve, step, root, var, tmp, eps):
    step(dve.reciprocal(root[:, :], root[:, :]))
    step(dve.tensor_tensor(tmp[:, :], root[:, :], root[:, :], ALU.mult))
    step(dve.scalar_tensor_tensor(out=tmp[:, :], in0=var, scalar=eps, in1=tmp[:, :], op0=ALU.add, op1=ALU.mult))
    step(dve.tensor_scalar(tmp[:, :], tmp[:, :], -0.5, 1.5, ALU.mult, ALU.add))
    step(dve.tensor_tensor(root[:, :], root[:, :], tmp[:, :], ALU.mult))


def project_and_pack(nc, a, scr):
    BITS = EC.bit_length() - 1
    ctx = ExitStack()
    with ctx:
        s = Space(nc, ctx, "qkv")
        x_in = [s.sb(f"x_in{i}", [P, TG, C]) for i in range(2)]
        x_norm = [s.sb(f"x_norm{i}", [P, TG, C]) for i in range(2)]
        stats = s.sb("stats", [P, TG, 6])
        mean_var = s.sb("mean_var", [P, TG, 2])
        rstd = s.sb("rstd", [P, TG])
        newton = s.sb("newton", [P, TG])
        ident = s.sb("ident", [P, P])
        xT = s.sb("xT", [P, CC, GT])
        w = [s.sb(f"w{i}", [P, CC, C]) for i in range(5)]
        bias = s.sb("bias", [P, 5, CC])
        bv_row = s.sb("bv_row", [P, C])
        cos = s.sb("cos", [P, N])
        sin = s.sb("sin", [P, N])
        sign = s.sb("sign", [P, 1])
        eps = s.sb("eps", [P, 1])
        lin = s.sb("lin", [P, 4, CC, GT])
        turned = [s.sb(f"turned{i}", [P, CC, GT]) for i in range(2)]
        tmp = s.sb("tmp", [P, CC, GT])
        hi = [[s.sb(f"hi{i}{j}", [P, CC, GT], F16) for j in range(2)] for i in range(2)]
        lo = [[s.sb(f"lo{i}{j}", [P, CC, GT], F16) for j in range(2)] for i in range(2)]
        v_chan = [s.sb(f"v_chan{i}", [P, CC, GT]) for i in range(2)]
        v_tok = s.sb("v_tok", [P, TG, C])
        v_stack = [s.sb(f"v_stack{i}", [P, TG, NH, VS], F16) for i in range(2)]
        zeros = s.sb("zeros", [P, PH * PW])
        key = s.sb("key", [P, EC], I32)
        src = s.sb("src", [P, EC], I32)
        way = src[:, 0:EC // 2].bitcast(I16)
        dropped = s.sb("dropped", [P, EC], I16)
        before = s.sb("before", [P, EC], I16)
        moves = before
        kept = s.sb("kept", [P, 1])
        most = s.sb("most", [P, 1])
        count = s.sb("count", [P, 2], I32)
        tail = s.sb("tail", [P, PAIR], I32)
        t_ps = s.ps("t_ps", [P, CC, 512])
        o_ps = s.ps("o_ps", [P, 6, 512])

        const_in = s.sem("const_in")
        const_ok = s.sem("const_ok")
        act_const = s.sem("act_const")
        ident_ok = s.sem("ident_ok")
        x_ready = [s.sem(f"x_ready{i}") for i in range(2)]
        x_free = s.sem("x_free")
        stats_ok = s.sem("stats_ok")
        root_ok = s.sem("root_ok")
        norm_ok = s.sem("norm_ok")
        norm_free = s.sem("norm_free")
        turn_done = s.sem("turn_done")
        xT_ok = s.sem("xT_ok")
        lin_done = s.sem("lin_done")
        lin_taken = s.sem("lin_taken")
        v_rows_taken = s.sem("v_rows_taken")
        turned_ok = s.sem("turned_ok")
        hi_ok = s.sem("hi_ok")
        parts_ok = s.sem("parts_ok")
        lin_free = s.sem("lin_free")
        v_tok_ok = s.sem("v_tok_ok")
        v_hi_ok = s.sem("v_hi_ok")
        v_ok = s.sem("v_ok")
        stored = [s.sem(f"stored{i}") for i in range(2)]
        zeroed = s.sem("zeroed")
        edge_in = s.sem("edge_in")
        pack_s = s.sem("pack_s")
        kept_ok = s.sem("kept_ok")
        most_ok = s.sem("most_ok")
        packed = s.sem("packed")
        keys_stored = s.sem("keys_stored")
        dve_s = s.sem("dve_s")
        passed = s.sem("passed")

        x_v = a["x"].rearrange("(g t p) c -> g p t c", t=TG, p=P)
        NCONST = 5 + 5 + 1 + 8 + 1
        STORES = 8 * CC + CC + TG
        DVE_PER = 2 * TG + 5

        block = ctx.enter_context(nc.Block())

        @block.sync
        def _(sp):
            for par in range(2):
                sp.sem_inc(stored[par], 16)
            for i, n in enumerate(["Wq", "Wq_swap", "Wk", "Wk_swap", "Wv"]):
                sp.dma_start(w[i][:, :, :], a[n].rearrange("(k p) n -> p k n", p=P)).then_inc(const_in, 16)
            for i, n in enumerate(["bq", "bq_swap", "bk", "bk_swap", "bv"]):
                sp.dma_start(bias[:, i, :], a[n]).then_inc(const_in, 16)
            sp.dma_start(bv_row[:, :], a["bv_row"].to_broadcast([P, C])).then_inc(const_in, 16)
            for r in range(P // HD):
                sp.dma_start(cos[r * HD:(r + 1) * HD, :], a["cos"]).then_inc(const_in, 16)
                sp.dma_start(sin[r * HD:(r + 1) * HD, :], a["sin"]).then_inc(const_in, 16)
            sp.dma_start(sign[:, :], a["sign"]).then_inc(const_in, 16)
            sp.dma_start(src[:, :], a["edges"][0].rearrange("(p e) -> p e", p=P)).then_inc(edge_in, 16)
            sp.dma_start(key[:, :], a["edges"][1].rearrange("(p e) -> p e", p=P)).then_inc(edge_in, 16)
            sp.wait_ge(zeroed, 1)
            for b in range(B):
                sp.dma_start(scr["v_pad"].rearrange("(m p) b n -> b p m n", p=P)[b],
                             zeros[:, None, :].to_broadcast([P, CC, PH * PW])).then_inc(zeroed, 16)
            sp.wait_ge(zeroed, 1 + 16 * B)
            sp.wait_ge(ident_ok, 4)
            with sp.Fori(0, B) as b:
                with sp.Fori(0, GI // 2) as gp:
                    for par in range(2):
                        g = b * GI + gp * 2 + par
                        tok = g * GT
                        for i, name in enumerate(["q_parts", "k_parts"]):
                            dst = scr[name].rearrange("(m h) (s d) n -> s m h d n", m=CC, d=HD)
                            sp.wait_ge(parts_ok, 2 * g + i + 1)
                            for sl, part in enumerate([hi, hi, lo, lo] if i == 0 else [hi, lo, hi, lo]):
                                for m in range(CC):
                                    sp.dma_start(dst[sl, m, :, :, bass.ds(tok, GT)], part[i][par][:, m, :])\
                                        .then_inc(stored[par], 16)
                        sp.wait_ge(v_ok, g + 1)
                        dst = scr["v_pad"].rearrange("(m p) b (r w) -> m p b r w", p=P, w=PW)
                        for m in range(CC):
                            sp.dma_start(dst[m, :, b, bass.ds(gp * 2 * GR + par * GR + 2, GR), 2:2 + W],
                                           v_chan[par][:, m, :].rearrange("p (r w) -> p r w", w=W))\
                                .then_inc(stored[par], 16)
                        dst = scr["v_stack"].rearrange("b h p (g k) -> b g p h k", k=TG * VS)
                        for t in range(TG):
                            sp.dma_start(dst[b, gp * 2 + par, :, :, t * VS:(t + 1) * VS],
                                           v_stack[par][:, t, :, :]).then_inc(stored[par], 16)
            for par in range(2):
                sp.wait_ge(stored[par], 16 + 16 * STORES * NG // 2)
            sp.wait_ge(packed, 1)
            sp.dma_start(scr["keys"][:, 0:EC], key[:, :]).then_inc(keys_stored, 16)
            sp.dma_start(scr["keys"][:, EC:EC + PAIR], tail[:, :]).then_inc(keys_stored, 16)
            sp.dma_start(scr["counts"], count[:, :]).then_inc(keys_stored, 16)
            sp.wait_ge(keys_stored, 48)

        @block.gpsimd
        def _(pool):
            make_identity(pool, ident, ident_ok)
            for i in range(2):
                pool.memset(v_stack[i][:, :, :, 2 * HD:], 1.0).then_inc(ident_ok, 1)
            with pool.Fori(0, NG // 2) as i:
                for par in range(2):
                    pool.wait_ge(x_free, 2 * i + par + 1)
                    pool.dma_start(x_in[par][:, :, :], x_v[2 * i + par]).then_inc(x_ready[par], 16)
            pool.wait_ge(x_free, NG + 1)
            pool.dma_start(x_in[0][:, :, :], x_v[0]).then_inc(x_ready[0], 16)
            pool.wait_ge(kept_ok, 1)
            pool.partition_all_reduce(most[:, :], kept[:, :], P, REDUCE_MAX).then_inc(most_ok, 1)

        @block.tensor
        def _(pe):
            pe.wait_ge(ident_ok, 2)
            pe.wait_ge(const_in, 16 * NCONST)
            pe.sem_inc(norm_free, 2)
            pe.sem_inc(lin_done, 12)
            with pe.Fori(0, NG // 2) as i:
                for par in range(2):
                    g = 2 * i + par
                    pe.wait_ge(norm_ok, g + 1)
                    pe.wait_ge(xT_ok, 2 + 2 * g)
                    for t in range(TG):
                        for m in range(CC):
                            last = pe.transpose(t_ps[:, m, t * P:(t + 1) * P], x_norm[par][:, t, m * P:(m + 1) * P],
                                                ident[:, :])
                    last.then_inc(turn_done, 1)
                    pe.wait_ge(turn_done, g + 1)
                    pe.sem_inc(norm_free, 1)
                    pe.wait_ge(xT_ok, 2 + 2 * g + 2)
                    for n in range(12):
                        bank = [0, 1, 2, 3, 0, 1, 2, 3, 4, 5, 4, 5][n]
                        if n < 8:
                            pe.wait_ge(lin_taken, 8 * g + 8 + n - 4 + 1)
                        else:
                            pe.wait_ge(v_rows_taken, 4 * g + 4 + n - 8 - 2 + 1)
                        if n < 10:
                            wi, m = (n % 4, n // 4) if n < 8 else (4, n - 8)
                            for k in range(CC):
                                last = pe.matmul(o_ps[:, bank, :GT], w[wi][:, k, m * P:(m + 1) * P], xT[:, k, :],
                                                 start=(k == 0), stop=(k == CC - 1))
                        else:
                            for t in ([0, 1] if n == 10 else [2]):
                                for k in range(CC):
                                    last = pe.matmul(o_ps[:, bank, (t % 2) * C:(t % 2 + 1) * C],
                                                     xT[:, k, t * P:(t + 1) * P], w[4][:, k, :],
                                                     start=(k == 0), stop=(k == CC - 1))
                        last.then_inc(lin_done, 1)

        @block.scalar
        def _(act):
            act.sem_inc(lin_taken, 8)
            act.sem_inc(xT_ok, 2)
            act.wait_ge(const_ok, 2)
            act.mul(bias[:, 2:4, :], bias[:, 2:4, :], HD ** -0.5).then_inc(act_const, 1)
            act.wait_ge(act_const, 1)
            act.wait_ge(stats_ok, 1)
            act.activation(rstd[:, :], mean_var[:, :, 1], ACT.Sqrt, bias=eps[:, :]).then_inc(root_ok, 1)
            with act.Fori(0, NG // 2) as i:
                for par in range(2):
                    g = 2 * i + par
                    act.wait_ge(stats_ok, g + 2)
                    act.activation(rstd[:, :], mean_var[:, :, 1], ACT.Sqrt, bias=eps[:, :]).then_inc(root_ok, 1)
                    act.wait_ge(turn_done, g + 1)
                    for m in range(CC):
                        if m == 0:
                            act.wait_ge(lin_done, 12 + 12 * g)
                        act.activation(xT[:, m, :], t_ps[:, m, :GT], ACT.Identity).then_inc(xT_ok, 1)
                    for n in range(8):
                        wi, m = n % 4, n // 4
                        act.wait_ge(lin_done, 12 + 12 * g + n + 1)
                        if n == 0:
                            act.wait_ge(lin_free, 2 + 2 * g)
                        act.activation(lin[:, wi, m, :], o_ps[:, wi, :GT], ACT.Identity, bias=bias[:, wi, m:m + 1],
                                       scale=1.0 if wi < 2 else HD ** -0.5).then_inc(lin_taken, 1)
                    act.wait_ge(stored[par], 16 + 16 * STORES * i)
                    for m in range(CC):
                        act.wait_ge(lin_done, 12 + 12 * g + 9 + m)
                        act.activation(v_chan[par][:, m, :], o_ps[:, 4 + m, :GT], ACT.Identity,
                                       bias=bias[:, 4, m:m + 1]).then_inc(v_rows_taken, 1)
                    for n in range(2):
                        act.wait_ge(turned_ok, 2 * g + n + 1)
                        act.activation(hi[n][par][:, :, :], turned[n][:, :, :], ACT.Identity).then_inc(hi_ok, 1)
                    act.wait_ge(v_tok_ok, g + 1)
                    act.activation(v_stack[par][:, :, :, 0:HD], v_tok[:, :, :].rearrange("p t (h d) -> p t h d", d=HD),
                                   ACT.Identity, scale=V_SCALE).then_inc(v_hi_ok, 1)

        @block.vector
        def _(dve):
            step = Steps(dve, dve_s)
            dve.sem_inc(x_free, 2)
            dve.sem_inc(lin_free, 2)
            dve.sem_inc(v_rows_taken, 4)
            dve.memset(zeros[:, :], 0.0).then_inc(zeroed, 1)
            dve.wait_ge(const_in, 16 * NCONST)
            dve.memset(eps[:, :], 1e-6).then_inc(const_ok, 1)
            dve.tensor_scalar(sin[:, :], sin[:, :], sign[:, 0:1], None, ALU.mult).then_inc(const_ok, 1)
            dve.wait_ge(const_ok, 2)

            def normalise(g, i, par, started):
                step.start, step.n = started, 0
                dve.wait_ge(x_ready[par], 16 * i + 16)
                layernorm_stats(dve, step, x_in[par], stats, mean_var, TG, passed)
                dve.sem_inc(stats_ok, 1)
                dve.wait_ge(root_ok, g + 1)
                reciprocal_root(dve, step, rstd, mean_var[:, :, 1], newton, 1e-6)
                dve.wait_ge(norm_free, g + 1)
                for t in range(TG):
                    last = dve.tensor_scalar(x_norm[par][:, t, :], x_in[par][:, t, :], mean_var[:, t, 0:1],
                                             rstd[:, t:t + 1], ALU.subtract, ALU.mult)
                last.then_inc(norm_ok, 1)
                dve.wait_ge(norm_ok, g + 1)
                dve.sem_inc(x_free, 1)

            pack = Steps(dve, pack_s)

            def edge_keys():
                dve.wait_ge(edge_in, 32)
                pack(dve.tensor_scalar(dropped[:, :], key[:, :], float(M), None, ALU.is_ge))
                pack(dve.tensor_tensor_scan(before[:, :], dropped[:, :], dropped[:, :], 0.0, ALU.add, ALU.max))
                pack(dve.tensor_scalar(src[:, :], src[:, :], float(M - 1), None, ALU.min))
                pack(dve.tensor_scalar(key[:, :], key[:, :], SRC_BITS, None, ALU.logical_shift_left))
                pack(dve.tensor_tensor(key[:, :], key[:, :], src[:, :], ALU.bitwise_or))
                dve.tensor_scalar(kept[:, :], before[:, EC - 1:EC], -1.0, float(EC), ALU.mult, ALU.add).then_inc(kept_ok, 1)
                pack(dve.scalar_tensor_tensor(out=way, in0=dropped[:, :], scalar=0.0, in1=before[:, :],
                                              op0=ALU.is_equal, op1=ALU.mult))
                dve.wait_ge(kept_ok, 1)

            def move_ways(bit):
                d = 1 << bit
                pack(dve.tensor_scalar(moves[:, :], way, d, None, ALU.bitwise_and))
                pack(dve.copy_predicated(way[:, 0:EC - d], moves[:, d:EC], way[:, d:EC]))

            def move_keys(bit):
                d = 1 << bit
                pack(dve.copy_predicated(key[:, 0:EC - d], moves[:, d:EC], key[:, d:EC]))

            normalise(0, 0, 0, 0)
            for g in range(NG):
                i, par = g // 2, g % 2
                normalise(g + 1, i + par, 1 - par, (g + 1) * DVE_PER + g * 5)
                step.start, step.n = (g + 2) * DVE_PER + g * 5, 0
                if g == 0:
                    edge_keys()
                elif g % 2 == 1:
                    move_ways(g // 2)
                else:
                    move_keys(g // 2 - 1)
                here = bass.ds(g % GI * GT, GT)
                dve.wait_ge(stored[par], 16 + 16 * STORES * i)
                for n in range(2):
                    dve.wait_ge(lin_taken, 8 * g + 8 + 6 + 2 * n)
                    dve.tensor_tensor(tmp[:, :, :], lin[:, 2 * n + 1, :, :],
                                      sin[:, None, here].to_broadcast([P, CC, GT]), ALU.mult)
                    step(dve.tensor_tensor(turned[n][:, :, :], lin[:, 2 * n, :, :],
                                           cos[:, None, here].to_broadcast([P, CC, GT]), ALU.mult))
                    dve.tensor_tensor(turned[n][:, :, :], turned[n][:, :, :], tmp[:, :, :],
                                      ALU.add).then_inc(turned_ok, 1)
                    dve.wait_ge(turned_ok, 2 * g + n + 1)
                    dve.sem_inc(lin_free, 1)
                dve.wait_ge(lin_done, 12 + 12 * g + 12)
                dve.tensor_tensor(v_tok[:, 0:2, :], o_ps[:, 4, :].rearrange("p (t c) -> p t c", t=2),
                                  bv_row[:, None, :].to_broadcast([P, 2, C]), ALU.add).then_inc(v_rows_taken, 1)
                dve.tensor_tensor(v_tok[:, 2, :], o_ps[:, 5, 0:C], bv_row[:, :], ALU.add)\
                    .then_inc(v_rows_taken, 1)
                dve.wait_ge(v_rows_taken, 4 * g + 8)
                dve.sem_inc(v_tok_ok, 1)
                for n in range(2):
                    dve.wait_ge(hi_ok, 2 * g + n + 1)
                    dve.tensor_tensor(lo[n][par][:, :, :], turned[n][:, :, :], hi[n][par][:, :, :],
                                      ALU.subtract).then_inc(parts_ok, 1)
                dve.wait_ge(parts_ok, 2 * g + 2)
                dve.wait_ge(v_hi_ok, g + 1)
                for t in range(TG):
                    step(dve.scalar_tensor_tensor(
                        out=v_stack[par][:, t, :, HD:2 * HD],
                        in0=v_tok[:, t, :].rearrange("p (h d) -> p h d", d=HD), scalar=V_SCALE,
                        in1=v_stack[par][:, t, :, 0:HD], op0=ALU.mult, op1=ALU.subtract))
                dve.sem_inc(v_ok, 1)
            move_keys(NG // 2 - 1)
            for bit in range(NG // 2, BITS):
                move_ways(bit)
                move_keys(bit)
            pack(dve.memset(tail[:, :], 0))
            dve.wait_ge(most_ok, 1)
            pack(dve.tensor_copy(count[:, 0:1], most[:, :]))
            dve.tensor_copy(count[:, 1:2], kept[:, :]).then_inc(packed, 1)


def attend(nc, a, scr):
    WHOLE = (4, 10, 16)
    UC = 9
    KC = N // 3
    EXP_LAG, TURN_LAG, AV_LAG = 4, 15, 4
    SPI = B * UC
    JPU, JPI = JM, B * JM
    ITER = NH * GI
    T_RING, PART_RING = 3, 9

    ctx = ExitStack()
    with ctx:
        s = Space(nc, ctx, "att")
        q_sb = [s.sb(f"q{b}", [P, GT], F16) for b in range(B)]
        k_sb = [s.sb(f"k{b}", [P, N], F16) for b in range(B)]
        v_sb = [s.sb(f"v{b}", [P, JM, VS], F16) for b in range(B)]
        mask = [s.sb(f"mask{t}", [P, N]) for t in range(TG)]
        prob = [s.sb(f"prob{b}", [P, TG, N]) for b in range(B)]
        row_max = [s.sb(f"row_max{i}", [P, TG, 3]) for i in range(2)]
        neg_max = [s.sb(f"neg_max{i}", [P, TG]) for i in range(2)]
        shift = s.sb("shift", [P, 3])
        junk = s.sb("junk", [P, 3])
        pair = [s.sb(f"pair{i}", [P, 2 * GT], F16) for i in range(PART_RING)]
        hi = [p[:, 0:GT] for p in pair]
        lo = [p[:, GT:] for p in pair]
        whole = [p[:, :].bitcast(F32) for p in pair]
        v_whole = [s.sb(f"v_whole{b}", [P, len(WHOLE), VS]) for b in range(B)]
        out_sb = [s.sb(f"out{i}", [VS, GT]) for i in range(2)]
        ident = s.sb("ident", [P, P])
        score_ps = [s.ps(f"score{i}", [P, 1024]) for i in range(2)]
        turn_ps = [s.ps(f"turn{i}", [P, 512]) for i in range(T_RING)]
        out_ps = s.ps("out_ps", [P, 512])

        ident_ok = s.sem("ident_ok")
        q_in = [s.sem(f"q_in{b}") for b in range(B)]
        k_in = [s.sem(f"k_in{b}") for b in range(B)]
        v_in = [s.sem(f"v_in{b}") for b in range(B)]
        mask_in = [s.sem(f"mask_in{t}") for t in range(TG)]
        score_done = s.sem("score_done")
        score_taken = s.sem("score_taken")
        max_ok = s.sem("max_ok")
        exp_ok = s.sem("exp_ok")
        turn_done = s.sem("turn_done")
        hi_ok = s.sem("hi_ok")
        lo_ok = s.sem("lo_ok")
        v_whole_ok = s.sem("v_whole_ok")
        av_done = s.sem("av_done")
        evac_ok = s.sem("evac_ok")
        stored = [s.sem(f"stored{i}") for i in range(2)]
        shift_ok = s.sem("shift_ok")
        passed = s.sem("passed")

        def splits(j):
            return j // JPU * (JPU - len(WHOLE)) + sum(1 for k in range(j % JPU) if k not in WHOLE)

        def wait_chunk(eng, it, j):
            if j % JPU in WHOLE:
                eng.wait_ge(hi_ok, it * JPI + j + 1)
            else:
                eng.wait_ge(lo_ok, it * splits(JPI) + splits(j + 1))

        block = ctx.enter_context(nc.Block())

        def loads(sp, h, g, new_head, first):
            it = h * GI + g
            for b in range(B):
                if b == 3:
                    for t in range(TG):
                        if not first:
                            sp.wait_ge(score_taken, 2 + SPI * it - UC + 3 * t + 3)
                        sp.dma_start(mask[t][:, :], a["mask"].rearrange("h (g t p) m -> h g t p m", t=TG, p=P)[h, g, t])\
                            .then_inc(mask_in[t], 16)
                if not first:
                    sp.wait_ge(score_done, SPI * it - SPI + UC * b + UC)
                sp.dma_start(q_sb[b][:, :], scr["q_parts"][h, :, bass.ds(g * GT + b * N, GT)]).then_inc(q_in[b], 16)
                if new_head:
                    sp.dma_start(k_sb[b][:, :], scr["k_parts"][h, :, b * N:(b + 1) * N]).then_inc(k_in[b], 16)
            if new_head:
                for b in range(B):
                    if not first:
                        sp.wait_ge(av_done, PART_RING + JPI * it - JPI + JPU * (b + 1))
                    sp.dma_start(v_sb[b][:, :, :], scr["v_stack"][b, h].rearrange("p (j v) -> p j v", v=VS))\
                        .then_inc(v_in[b], 16)

        @block.sync
        def _(sp):
            loads(sp, 0, 0, True, True)
            with sp.Fori(1, GI) as g:
                loads(sp, 0, g, False, False)
            with sp.Fori(1, NH) as h:
                loads(sp, h, 0, True, False)
                with sp.Fori(1, GI) as g:
                    loads(sp, h, g, False, False)

        @block.gpsimd
        def _(pool):
            make_identity(pool, ident, ident_ok)
            for b in range(B):
                pool.memset(v_whole[b][:, :, HD:2 * HD], 0.0)
                pool.memset(v_whole[b][:, :, 2 * HD:], 1.0)

            def unit(h, g, b):
                u = (h * GI + g) * B + b
                pool.wait_ge(evac_ok, u + 1)
                dst = scr["att"].rearrange("k (h d) n -> h k d n", d=HD)
                for k in range(2):
                    pool.dma_start(dst[h, k, :, bass.ds(g * GT + b * N, GT)],
                                   out_sb[b % 2][k * HD:(k + 1) * HD, :]).then_inc(stored[b % 2], 16)
                pool.dma_start(scr["att_sum"][bass.ds(h, 1), bass.ds(g * GT + b * N, GT)],
                               out_sb[b % 2][2 * HD:2 * HD + 1, :]).then_inc(stored[b % 2], 16)

            with pool.Fori(0, NH) as h:
                for b in range(B):
                    pool.wait_ge(v_in[b], h * 16 + 16)
                    for i, j in enumerate(WHOLE):
                        last = pool.tensor_tensor(v_whole[b][:, i, 0:HD], v_sb[b][:, j, 0:HD], v_sb[b][:, j, HD:2 * HD],
                                                  ALU.add)
                    last.then_inc(v_whole_ok, 1)
                with pool.Fori(0, GI) as g:
                    for b in range(B):
                        unit(h, g, b)
            for i in range(2):
                pool.wait_ge(stored[i], 48 * ITER * B // 2)

        def multiply(pe, h, new_head, it, j):
            ab, aj = j // JPU % B, j % JPU
            if aj == 0:
                pe.wait_ge(v_in[ab], h * 16 + (0 if new_head and j < 0 else 16))
                if not (isinstance(it, int) and it * B + j // JPU == 0):
                    pe.wait_ge(evac_ok, it * B + j // JPU)
            wait_chunk(pe, it, j)
            if aj in WHOLE:
                if aj == WHOLE[0]:
                    pe.wait_ge(v_whole_ok, h * B + (B if not new_head else ab + 1 if j >= 0 else 0))
                last = pe.matmul(out_ps[:VS, :GT], v_whole[ab][:, WHOLE.index(aj), :],
                                 whole[aj % PART_RING], start=(aj == 0), stop=(aj == JPU - 1))
            else:
                for part in (hi, lo):
                    last = pe.matmul(out_ps[:VS, :GT], v_sb[ab][:, aj, :], part[aj % PART_RING],
                                     start=(aj == 0 and part is hi), stop=(aj == JPU - 1 and part is lo))
            last.then_inc(av_done, 1)

        def pe_steps(pe, h, g, new_head, it, ks):
            static = isinstance(it, int)
            for k in ks:
                b, c = k // UC, k % UC
                if not (static and it >= ITER):
                    t, part = c // 3, c % 3
                    if c == 0:
                        pe.wait_ge(q_in[b], it * 16 + 16)
                        pe.wait_ge(k_in[b], h * 16 + 16)
                    pe.wait_ge(score_taken, it * SPI + k + 1)
                    for c0, n in ((0, 512), (512, KC - 512)):
                        last = pe.matmul(score_ps[k % 2][:, c0:c0 + n], q_sb[b][:, t * P:(t + 1) * P],
                                         k_sb[b][:, part * KC + c0:part * KC + c0 + n], start=True, stop=True)
                    last.then_inc(score_done, 1)
                for jj in range(2):
                    j = 2 * (k - TURN_LAG) + jj
                    if not (static and not 0 <= it * JPI + j < ITER * JPI):
                        tb, tj = j // JPU % B, j % JPU
                        if tj == 0:
                            pe.wait_ge(exp_ok, it * SPI + (j // JPU) * UC + UC)
                        if not (static and it * JPI + j < T_RING):
                            wait_chunk(pe, it, j - T_RING)
                        for t in range(TG):
                            last = pe.transpose(turn_ps[tj % T_RING][:, t * P:(t + 1) * P],
                                                prob[tb][:, t, tj * P:(tj + 1) * P], ident[:, :])
                        last.then_inc(turn_done, 1)
                    j -= AV_LAG
                    if not (static and not 0 <= it * JPI + j < ITER * JPI) and j % JPU > 0:
                        if j % JPU == 1:
                            multiply(pe, h, new_head, it, j - 1)
                        multiply(pe, h, new_head, it, j)

        DRAIN = range(0, TURN_LAG + (AV_LAG + 1) // 2)

        @block.tensor
        def _(pe):
            pe.sem_inc(turn_done, JPI)
            pe.sem_inc(av_done, PART_RING)
            pe.wait_ge(ident_ok, 2)
            pe_steps(pe, 0, 0, True, 0, range(SPI))
            with pe.Fori(1, GI) as g:
                pe_steps(pe, 0, g, False, g, range(SPI))
            with pe.Fori(1, NH) as h:
                pe_steps(pe, h, 0, True, h * GI, range(SPI))
                with pe.Fori(1, GI) as g:
                    pe_steps(pe, h, g, False, h * GI + g, range(SPI))
            pe_steps(pe, NH, 0, True, ITER, DRAIN)

        def act_steps(act, it, ks):
            static = isinstance(it, int)
            for k in ks:
                e = k - EXP_LAG
                if not (static and not 0 <= it * SPI + e < ITER * SPI):
                    b, c = e // UC % B, e % UC
                    t, part = c // 3, c % 3
                    if part == 0:
                        act.wait_ge(max_ok, it * B * TG + e // 3 + 1)
                    span = prob[b][:, t, part * KC:(part + 1) * KC]
                    act.activation(span, span, ACT.Exp, bias=neg_max[b % 2][:, t:t + 1]).then_inc(exp_ok, 1)
                for jj in range(2):
                    j = 2 * (k - TURN_LAG) + jj
                    if not (static and not 0 <= it * JPI + j < ITER * JPI + AV_LAG):
                        tj = j % JPU
                        if not (static and not 0 <= it * JPI + j < ITER * JPI):
                            act.wait_ge(turn_done, JPI + it * JPI + j + 1)
                            act.wait_ge(av_done, it * JPI + j + 1)
                            part = (whole if tj in WHOLE else hi)[tj % PART_RING]
                            act.activation(part[:, :], turn_ps[tj % T_RING][:, :GT], ACT.Identity)\
                                .then_inc(hi_ok, 1)
                        if tj == AV_LAG - 1 and not (static and it * JPI + j < JPU):
                            u = j // JPU - 1
                            ub = u % B
                            act.wait_ge(av_done, PART_RING + it * JPI + (u + 1) * JPU)
                            act.wait_ge(stored[ub % 2], 48 * (it * 2 + u // 2))
                            act.activation(out_sb[ub % 2][:, :], out_ps[:VS, :GT], ACT.Identity).then_inc(evac_ok, 1)

        @block.scalar
        def _(act):
            act_steps(act, 0, range(SPI))
            with act.Fori(1, ITER) as it:
                act_steps(act, it, range(SPI))
            act_steps(act, ITER, DRAIN)

        def dve_steps(dve, it, ks):
            static = isinstance(it, int)
            for k in ks:
                b, c = k // UC, k % UC
                if not (static and it >= ITER):
                    t, part = c // 3, c % 3
                    if b == 0 and part == 0:
                        dve.wait_ge(mask_in[t], it * 16 + 16)
                    dve.wait_ge(score_done, it * SPI + k + 1)
                    dve.wait_ge(turn_done, it * JPI + b * JPU + (part + 1) * JPU // 3)
                    part_wait(dve, passed)
                    dve.tensor_tensor_reduce(out=prob[b][:, t, part * KC:(part + 1) * KC],
                                             in0=score_ps[k % 2][:, :KC], in1=mask[t][:, part * KC:(part + 1) * KC],
                                             scale=1.0, scalar=-3e38, op0=ALU.add, op1=ALU.max,
                                             accum_out=row_max[b % 2][:, t, part:part + 1]).then_inc(score_taken, 1)
                    if part == 2:
                        dve.wait_ge(score_taken, 2 + it * SPI + k + 1)
                        part_wait(dve, passed)
                        dve.tensor_tensor_reduce(out=junk[:, :], in0=row_max[b % 2][:, t, :], in1=shift[:, :],
                                                 scale=-1.0, scalar=3e38, op0=ALU.add, op1=ALU.min,
                                                 accum_out=neg_max[b % 2][:, t:t + 1]).then_inc(max_ok, 1)
                for jj in range(2):
                    j = 2 * (k - TURN_LAG) + jj
                    if not (static and not 0 <= it * JPI + j < ITER * JPI) and j % JPU not in WHOLE:
                        tj = j % JPU
                        dve.wait_ge(hi_ok, it * JPI + j + 1)
                        dve.tensor_tensor(lo[tj % PART_RING][:, :], turn_ps[tj % T_RING][:, :GT],
                                          hi[tj % PART_RING][:, :], ALU.subtract).then_inc(lo_ok, 1)

        @block.vector
        def _(dve):
            dve.sem_inc(score_taken, 2)
            dve.memset(shift[:, :], -P_SHIFT).then_inc(shift_ok, 1)
            dve.wait_ge(shift_ok, 1)
            dve_steps(dve, 0, range(SPI))
            with dve.Fori(1, ITER) as it:
                dve_steps(dve, it, range(SPI))
            dve_steps(dve, ITER, DRAIN)


def mix_and_normalise(nc, a, scr):
    TAPS = 25
    PE_TAPS = list(range(13, TAPS))
    DVE_TAPS = list(range(13))
    EARLY = 3
    WIN = (GR + 4) * PW
    NP = len(PE_TAPS)
    ctx = ExitStack()
    with ctx:
        s = Space(nc, ctx, "mix")
        att = [s.sb(f"att{i}", [P, 3, CC, GT]) for i in range(2)]
        denom = s.sb("denom", [P, NH * M // P])
        win = [s.sb(f"win{i}", [P, CC, WIN]) for i in range(2)]
        x_res = [s.sb(f"x_res{i}", [P, TG, C]) for i in range(2)]
        acc = s.sb("acc", [P, CC, GT])
        yT = [s.sb(f"yT{i}", [P, CC, GT]) for i in range(2)]
        x2 = [s.sb(f"x2{i}", [P, TG, C]) for i in range(2)]
        x_norm = s.sb("x_norm", [P, TG, C])
        tT = [s.sb(f"tT{i}", [P, CC, GT]) for i in range(2)]
        node = [s.sb(f"node{i}", [P, TG, HF + 2 * GHD]) for i in range(2)]
        prod = s.sb("prod", [P, 2, TG, HF])
        stats = s.sb("stats", [P, TG, 6])
        mean_var = s.sb("mean_var", [P, TG, 2])
        rstd = s.sb("rstd", [P, TG])
        newton = s.sb("newton", [P, TG])
        eps = s.sb("eps", [P, 1])
        ident = s.sb("ident", [P, P])
        diag = s.sb("diag", [P, CC, NP, P])
        taps = s.sb("taps", [P, CC, TAPS])
        dw_b = s.sb("dw_b", [P, CC])
        wo = s.sb("wo", [P, CC, C])
        bo_row = s.sb("bo_row", [P, C])
        w_gat = s.sb("w_gat", [P, CC, HF])
        att_rows = s.sb("att_rows", [P, 2, HF])
        conv_ps = [s.ps(f"conv{m}", [P, 512]) for m in range(CC)]
        o_ps = s.ps("o_ps", [P, 4, C])
        t_ps = s.ps("t_ps", [P, CC, 512])
        h_ps = s.ps("h_ps", [P, TG, HF])

        ident_ok = s.sem("ident_ok")
        const_in = s.sem("const_in")
        const_ok = s.sem("const_ok")
        in_ready = [s.sem(f"in_ready{i}") for i in range(2)]
        in_free = s.sem("in_free")
        denom_in = s.sem("denom_in")
        denom_ok = s.sem("denom_ok")
        x_ready = s.sem("x_ready")
        x_free = s.sem("x_free")
        x_res_ok = s.sem("x_res_ok")
        conv_done = s.sem("conv_done")
        yT_ok = s.sem("yT_ok")
        o_done = s.sem("o_done")
        x2_ok = s.sem("x2_ok")
        stats_ok = s.sem("stats_ok")
        root_ok = s.sem("root_ok")
        norm_ok = s.sem("norm_ok")
        turn_done = s.sem("turn_done")
        tT_ok = s.sem("tT_ok")
        h_done = s.sem("h_done")
        node_ok = s.sem("node_ok")
        stored = [s.sem(f"stored{i}") for i in range(2)]
        dve_s = s.sem("dve_s")
        passed = s.sem("passed")

        NCONST = 8
        x_v = a["x"].rearrange("(g t p) c -> g p t c", t=TG, p=P)
        x2_v = scr["x2"].rearrange("(g t p) c -> g p t c", t=TG, p=P)
        node_v = scr["nodes"].rearrange("(g t p) f -> g p t f", t=TG, p=P)
        tT_v = scr["tT"].rearrange("(m p) n -> p m n", p=P)

        block = ctx.enter_context(nc.Block())

        @block.sync
        def _(sp):
            sp.dma_start(taps[:, :, :], a["dw_w"]).then_inc(const_in, 16)
            sp.dma_start(dw_b[:, :], a["dw_b"]).then_inc(const_in, 16)
            sp.dma_start(wo[:, :, :], a["Wo"].rearrange("(k p) n -> p k n", p=P)).then_inc(const_in, 16)
            sp.dma_start(bo_row[:, :], a["bo_row"].to_broadcast([P, C])).then_inc(const_in, 16)
            sp.dma_start(w_gat[:, :, :], a["W_gat"].rearrange("(k p) n -> p k n", p=P)).then_inc(const_in, 16)
            sp.dma_start(att_rows[:, 0, :], a["att_src"].to_broadcast([P, HF])).then_inc(const_in, 16)
            sp.dma_start(att_rows[:, 1, :], a["att_dst"].to_broadcast([P, HF])).then_inc(const_in, 16)
            sp.dma_start(eps[:, :], a["ln_eps"].to_broadcast([P, 1])).then_inc(const_in, 16)

            sp.dma_start(denom[:, :], scr["att_sum"].rearrange("h (q n) -> (h q) n", q=P // NH)).then_inc(denom_in, 16)
            sp.wait_ge(denom_ok, 1)
            sp.dma_start(scr["denom"].rearrange("h (q n) -> (h q) n", q=P // NH), denom[:, :]).then_inc(denom_in, 16)
            sp.wait_ge(denom_in, 32)

            def load(b, gi, g, par):
                for k in range(2):
                    sp.dma_start(att[par][:, k, :, :],
                                 scr["att"].rearrange("k (m p) n -> k p m n", p=P)[k, :, :, bass.ds(g * GT, GT)])\
                        .then_inc(in_ready[par], 16)
                for m in range(CC):
                    sp.dma_start(att[par][:, 2, m, :],
                                 scr["denom"].rearrange("(m h) n -> m h n", m=CC)[m, :, None, bass.ds(g * GT, GT)]
                                 .to_broadcast([P // HD, HD, GT])).then_inc(in_ready[par], 16)
                sp.dma_start(win[par][:, :, :],
                             scr["v_pad"].rearrange("(m p) b n -> b p m n", p=P)[b, :, :, bass.ds(gi * (GR * PW), WIN)])\
                    .then_inc(in_ready[par], 16)

            with sp.Fori(0, B) as b:
                with sp.Fori(0, GI // 2) as gp:
                    for par in range(2):
                        sp.wait_ge(in_free, b * GI + gp * 2 + par + 1)
                        load(b, gp * 2 + par, b * GI + gp * 2 + par, par)
            sp.wait_ge(in_free, NG + 1)
            load(0, 0, 0, 0)

        @block.gpsimd
        def _(pool):
            make_identity(pool, ident, ident_ok)
            pool.wait_ge(const_in, 16 * NCONST)
            with pool.Fori(0, NG // 2) as i:
                for par in range(2):
                    g = 2 * i + par
                    pool.wait_ge(x_free, g + 1)
                    pool.dma_start(x_res[par][:, :, :], x_v[g]).then_inc(x_ready, 16)
                    pool.wait_ge(x_ready, 16 * g + 16)
                    pool.tensor_tensor(x_res[par][:, :, :], x_res[par][:, :, :],
                                       bo_row[:, None, :].to_broadcast([P, TG, C]), ALU.add).then_inc(x_res_ok, 1)

        def pairs(eng, step, last):
            for par in range(2):
                step(par, 0, par, par == 0)
            with eng.Fori(1, NG // 2) as i:
                for par in range(2):
                    step(2 * i + par, i, par, False)
            last()

        @block.scalar
        def _(act):
            def turn(g, par):
                act.wait_ge(turn_done, g + 1)
                for m in range(CC):
                    act.activation(tT[par][:, m, :], t_ps[:, m, :GT], ACT.Identity).then_inc(tT_ok, 1)
                act.wait_ge(tT_ok, 2 * g + 2)
                act.dma_start(tT_v[:, :, bass.ds(g * GT, GT)], tT[par][:, :, :]).then_inc(stored[par], 16)

            def store_nodes(g, par):
                act.wait_ge(node_ok, g + 1)
                act.dma_start(node_v[g], node[par][:, :, :]).then_inc(stored[par], 16)

            def one(g, i, par, first):
                if not first:
                    turn(g - 1, 1 - par)
                act.wait_ge(x2_ok, g + 1)
                act.dma_start(x2_v[g], x2[par][:, :, :]).then_inc(stored[par], 16)
                act.wait_ge(stats_ok, g + 1)
                act.activation(rstd[:, :], mean_var[:, :, 1], ACT.Sqrt, bias=eps[:, :]).then_inc(root_ok, 1)
                if not first:
                    store_nodes(g - 1, 1 - par)

            def close():
                turn(NG - 1, 1)
                store_nodes(NG - 1, 1)

            pairs(act, one, close)
            for par in range(2):
                act.wait_ge(stored[par], 48 * NG // 2)

        @block.tensor
        def _(pe):
            def conv(g, i, par):
                pe.wait_ge(in_ready[par], 80 * i + 80)
                for m in range(CC):
                    view = win[par][:, m, :].rearrange("p (r w) -> p r w", w=PW)
                    for n, q in enumerate(PE_TAPS):
                        last = pe.matmul(conv_ps[m][:, :GT], diag[:, m, n, :],
                                         view[:, q // 5:q // 5 + GR, q % 5:q % 5 + W],
                                         start=(n == 0), stop=(n == NP - 1))
                last.then_inc(conv_done, 1)

            def turn(g, par):
                pe.wait_ge(norm_ok, g + 1)
                for t in range(TG):
                    for m in range(CC):
                        last = pe.transpose(t_ps[:, m, t * P:(t + 1) * P], x_norm[:, t, m * P:(m + 1) * P], ident[:, :])
                last.then_inc(turn_done, 1)
                pe.wait_ge(tT_ok, 2 * g + 2)
                for t in range(TG):
                    for k in range(CC):
                        last = pe.matmul(h_ps[:, t, :], tT[par][:, k, t * P:(t + 1) * P], w_gat[:, k, :],
                                         start=(k == 0), stop=(k == CC - 1))
                last.then_inc(h_done, 1)

            def one(g, i, par, first):
                pe.wait_ge(yT_ok, 2 * g + 2)
                if not first:
                    pe.wait_ge(x2_ok, g)
                for t in range(TG):
                    for k in range(CC):
                        last = pe.matmul(o_ps[:, t, :], yT[par][:, k, t * P:(t + 1) * P], wo[:, k, :],
                                         start=(k == 0), stop=(k == CC - 1))
                last.then_inc(o_done, 1)
                if not first:
                    turn(g - 1, 1 - par)
                conv(g + 1, i + par, 1 - par)

            pe.wait_ge(const_ok, 1)
            pe.wait_ge(const_in, 16 * NCONST)
            conv(0, 0, 0)
            pairs(pe, one, lambda: turn(NG - 1, 1))

        @block.vector
        def _(dve):
            step = Steps(dve, dve_s)
            dve.sem_inc(in_free, 2)
            dve.sem_inc(x_free, 2)
            dve.wait_ge(denom_in, 16)
            step(dve.reciprocal(denom[:, :], denom[:, :]))
            dve.sem_inc(denom_ok, 1)
            dve.wait_ge(const_in, 16 * NCONST)
            dve.wait_ge(ident_ok, 2)
            for m in range(CC):
                for n, q in enumerate(PE_TAPS):
                    last = dve.tensor_scalar(diag[:, m, n, :], ident[:, :], taps[:, m, q:q + 1], None, ALU.mult)
            last.then_inc(const_ok, 1)

            def add_taps(par, taps_of):
                for q in taps_of:
                    for m in range(CC):
                        view = win[par][:, m, :].rearrange("p (r w) -> p r w", w=PW)
                        sums = acc[:, m, :].rearrange("p (r w) -> p r w", w=W)
                        step(dve.scalar_tensor_tensor(out=sums, in0=view[:, q // 5:q // 5 + GR, q % 5:q % 5 + W],
                                                      scalar=taps[:, m, q:q + 1], in1=sums,
                                                      op0=ALU.mult, op1=ALU.add), lag=1)
                step.wait()

            def begin_mix(i, par):
                dve.wait_ge(in_ready[par], 80 * i + 80)
                step(dve.tensor_tensor(att[par][:, 0, :, :], att[par][:, 0, :, :], att[par][:, 1, :, :], ALU.add))
                step(dve.scalar_tensor_tensor(out=acc[:, :, :], in0=att[par][:, 0, :, :], scalar=1.0 / V_SCALE,
                                              in1=att[par][:, 2, :, :], op0=ALU.mult, op1=ALU.mult))
                add_taps(par, DVE_TAPS[:EARLY])

            def end_mix(g, par):
                add_taps(par, DVE_TAPS[EARLY:])
                dve.wait_ge(conv_done, g + 1)
                for m in range(CC):
                    dve.scalar_tensor_tensor(out=yT[par][:, m, :], in0=conv_ps[m][:, :GT], scalar=dw_b[:, m:m + 1],
                                             in1=acc[:, m, :], op0=ALU.add, op1=ALU.add).then_inc(yT_ok, 1)
                dve.wait_ge(yT_ok, 2 * g + 2)
                dve.sem_inc(in_free, 1)

            def features(g, par):
                dve.wait_ge(h_done, g + 1)
                dve.tensor_copy(node[par][:, :, 0:HF], h_ps[:, :, :])
                for k in range(2):
                    step(dve.tensor_tensor(prod[:, k, :, :], h_ps[:, :, :],
                                           att_rows[:, k, None, :].to_broadcast([P, TG, HF]), ALU.mult))
                for k in range(2):
                    last = dve.tensor_reduce(node[par][:, :, HF + k * GHD:HF + (k + 1) * GHD],
                                             prod[:, k, :, :].rearrange("p t (h x) -> p t h x", x=NX), AX.X, ALU.add)
                last.then_inc(node_ok, 1)

            begin_mix(0, 0)
            end_mix(0, 0)
            MIX = step.n
            FEATURES = 2
            PER = (MIX - 1) + 2 * TG + 5 + FEATURES

            def one(g, i, par, first):
                step.start, step.n = MIX + g * PER - (0 if first else FEATURES), 0
                begin_mix(i + par, 1 - par)
                dve.wait_ge(o_done, g + 1)
                dve.wait_ge(x_res_ok, g + 1)
                if not (isinstance(i, int) and i == 0):
                    dve.wait_ge(stored[par], 48 * i)
                dve.tensor_tensor(x2[par][:, :, :], o_ps[:, 0:TG, :], x_res[par][:, :, :], ALU.add).then_inc(x2_ok, 1)
                dve.wait_ge(x2_ok, g + 1)
                dve.sem_inc(x_free, 1)
                layernorm_stats(dve, step, x2[par], stats, mean_var, TG, passed)
                dve.sem_inc(stats_ok, 1)
                if not first:
                    features(g - 1, 1 - par)
                end_mix(g + 1, 1 - par)
                dve.wait_ge(root_ok, g + 1)
                reciprocal_root(dve, step, rstd, mean_var[:, :, 1], newton, LN_EPS)
                for t in range(TG):
                    last = dve.tensor_scalar(x_norm[:, t, :], x2[par][:, t, :], mean_var[:, t, 0:1],
                                             rstd[:, t:t + 1], ALU.subtract, ALU.mult)
                last.then_inc(norm_ok, 1)
                assert step.n == PER - (FEATURES if first else 0)

            def close():
                step.start, step.n = MIX + NG * PER - FEATURES, 0
                features(NG - 1, 1)

            pairs(dve, one, close)


def aggregate(nc, a, scr):
    B_RING = 8
    HIDE_AT, OUT_AT, TAKE_AT = (0, 5), (3, 8), (11, 15)
    INDEX_AT = 4
    RANGE, FEATURE = 8.0, 16.0
    SCALE = float(np.log(64.0))
    AROWS = LO * TR
    NF = HF + 2 * GHD
    DT = 2 * GHD
    BLK = HI // P
    ctx = ExitStack()
    with ctx:
        s = Space(nc, ctx, "gat")
        nodes = s.sb("nodes", [P, NTILE, NF])
        dst_rows = s.sb("dst_rows", [P, NTILE, DT])
        work = [s.sb(f"work{i}", [P, NTILE, HF]) for i in range(2)]
        loops = s.sb("loops", [P, NTILE, TR])
        sums = s.sb("sums", [P, NTILE, TR])
        peak = s.sb("peak", [P, GHD])
        keys = [s.sb(f"keys{i}", [P, ET], I32) for i in range(2)]
        src_i = [s.sb(f"src_i{i}", [P, ET], I32) for i in range(2)]
        dst_i = [s.sb(f"dst_i{i}", [P, ET], I32) for i in range(2)]
        inside = [s.sb(f"inside{i}", [P, ET]) for i in range(2)]
        left = s.sb("left", [P, 1])
        counts = s.sb("counts", [P, 2], I32)
        lo = s.sb("lo", [P, ET])
        hi = s.sb("hi", [P, ET])
        g_src = [s.sb(f"g_src{i}", [P, ET, NF]) for i in range(2)]
        g_dst = [s.sb(f"g_dst{i}", [P, ET, DT]) for i in range(2)]
        logit = s.sb("logit", [P, ET, GHD])
        logit2 = s.sb("logit2", [P, ET, GHD])
        val = s.sb("val", [P, ET, TR])
        rest = s.sb("rest", [P, ET, TR])
        part = [s.sb(f"part{i}", [P, ET, TR], F16) for i in range(3)]
        one_lo = s.sb("one_lo", [P, ET, LO], F16)
        spread = [[s.sb(f"spread{i}{k}", [P, ET, LO, TR], F16) for k in range(3)] for i in range(2)]
        one_hi = [s.sb(f"one_hi{i}", [P, HI], F16) for i in range(B_RING)]
        iota_i = s.sb("iota_i", [P, HI], I32)
        iota_hi = s.sb("iota_hi", [P, HI], F16)
        iota_f = s.sb("iota_f", [P, ET])
        zeros = s.sb("zeros", [P, 512], F16)
        limits = s.sb("limits", [P, 2])
        wide = s.sb("wide", [P, 1], I32)
        w1 = s.sb("w1", [P, CC, NX, GF])
        w2 = s.sb("w2", [P, NX, FC, C])
        b1 = s.sb("b1", [P, NX, FC])
        b2_row = s.sb("b2_row", [P, NX, C])
        tT = s.sb("tT", [P, CC, FT])
        hidden = s.sb("hidden", [P, FC, FT])
        y = [s.sb(f"y{i}", [P, FG, C]) for i in range(2)]
        ident = s.sb("ident", [P, P])
        acc_sb = s.sb("acc_sb", [AROWS, HI])
        b_gat = s.sb("b_gat", [P, HF])
        gamma = s.sb("gamma", [P, HF])
        beta = s.sb("beta", [P, HF])
        small = [s.sb(f"small{i}", [P, NTILE]) for i in range(4)]
        score = s.sb("score", [P, NTILE, NX])
        rank = s.sb("rank", [P, NTILE, NX])
        gates = s.sb("gates", [P, NTILE, NX])
        eps = s.sb("eps", [P, 1])
        acc = s.ps("acc", [P, 3, 512])
        h_ps = s.ps("h_ps", [P, FC, 512])
        y_ps = s.ps("y_ps", [P, FG, C])

        weights_in = s.sem("weights_in")
        t_in = s.sem("t_in")
        h_done = s.sem("h_done")
        gelu_ok = s.sem("gelu_ok")
        y_done = s.sem("y_done")
        y_taken = s.sem("y_taken")
        y_stored = [s.sem(f"y_stored{i}") for i in range(2)]
        ident_ok = s.sem("ident_ok")
        const_in = s.sem("const_in")
        limit_ok = s.sem("limit_ok")
        limit_all = s.sem("limit_all")
        wide_ok = s.sem("wide_ok")
        dve_s = s.sem("dve_s")
        passed = s.sem("passed")
        peak_ok = s.sem("peak_ok")
        peak_all = s.sem("peak_all")
        table_ok = s.sem("table_ok")
        table_out = s.sem("table_out")
        exp_in = s.sem("exp_in")
        exp_out = s.sem("exp_out")
        keys_in = [s.sem(f"keys_in{i}") for i in range(2)]
        keys_free = s.sem("keys_free")
        decoded = s.sem("decoded")
        src_got = [s.sem(f"src_got{i}") for i in range(2)]
        dst_got = [s.sem(f"dst_got{i}") for i in range(2)]
        logit_ok = s.sem("logit_ok")
        weight_ok = s.sem("weight_ok")
        spread_ok = s.sem("spread_ok")
        one_ok = s.sem("one_ok")
        tile_done = s.sem("tile_done")
        acc_done = s.sem("acc_done")
        evac_ok = s.sem("evac_ok")
        block_turned = s.sem("block_turned")
        block_taken = s.sem("block_taken")
        root_in = s.sem("root_in")
        root_out = s.sem("root_out")
        tail_s = s.sem("tail_s")
        done = s.sem("done")
        stored = s.sem("stored")

        block = ctx.enter_context(nc.Block())

        def edge_loop(eng, body, group=None):
            most = eng.value_load(counts[0:1, 0:1], min_val=0, max_val=EC)
            with eng.Fori(0, NFG) as c:
                with eng.If(c * PAIR < most):
                    body(c, True)
                if group is not None:
                    with eng.If(c * PAIR >= most):
                        group(c)
            with eng.If(most > NFG * PAIR):
                with eng.Fori(0, OUTER) as o:
                    with eng.If((o * INNER + NFG) * PAIR < most):
                        with eng.Fori(0, INNER) as n:
                            with eng.If((o * INNER + n + NFG) * PAIR < most):
                                body(o * INNER + n + NFG, False)

        def by_range(eng, loop):
            eng.wait_ge(wide_ok, 1)
            is_wide = eng.value_load(wide[0:1, 0:1], min_val=0, max_val=1)
            with eng.If(is_wide < 1):
                loop(2, F16)
            with eng.If(is_wide >= 1):
                loop(3, BF16)

        @block.sync
        def _(sp):
            sp.dma_start(counts[:, :], scr["counts"]).then_inc(const_in, 16)
            sp.dma_start(nodes[:, :, :], scr["nodes"].rearrange("(t p) f -> p t f", p=P)).then_inc(const_in, 16)
            for dst, n in ((b_gat, "b_gat"), (gamma, "ln_gamma"), (beta, "ln_beta")):
                sp.dma_start(dst[:, :], a[n].to_broadcast([P, HF])).then_inc(const_in, 16)
            sp.dma_start(eps[:, :], a["ln_eps"].to_broadcast([P, 1])).then_inc(const_in, 16)
            sp.wait_ge(table_ok, 1)
            sp.dma_start(scr["dst_table"].rearrange("(t p) f -> p t f", p=P), dst_rows[:, :, :]).then_inc(table_out, 16)
            sp.wait_ge(const_in, 96)
            for i in range(2):
                sp.dma_start(keys[i][:, :], scr["keys"][:, i * ET:(i + 1) * ET]).then_inc(keys_in[i], 16)

            for k in range(CC):
                sp.dma_start(w1[:, k, :, :], a["W1"].rearrange("x (k p) f -> k p x f", p=P)[k]).then_inc(weights_in, 16)
            for x in range(NX):
                sp.dma_start(w2[:, x, :, :], a["W2"][x].rearrange("(k p) c -> p k c", p=P)).then_inc(weights_in, 16)
                sp.dma_start(b2_row[:, x, :], a["b2"][x:x + 1, :].to_broadcast([P, C])).then_inc(weights_in, 16)
            sp.dma_start(b1[:, :, :], a["b1"]).then_inc(weights_in, 16)
            for i in range(2):
                sp.sem_inc(y_stored[i], 16)

            def load_group(g):
                sp.wait_ge(h_done, NX * FC * (g + 1))
                sp.dma_start(tT[:, :, :], scr["tT"].rearrange("(m p) n -> p m n", p=P)[:, :, bass.ds(g * FT, FT)])\
                    .then_inc(t_in, 16)

            def store_output(g, e):
                sp.wait_ge(y_taken, 1 + g * NX + e + 1)
                sp.dma_start(scr["y"][g, e], y[e % 2][:, :, :].rearrange("p t c -> p (t c)")).then_inc(y_stored[e % 2], 16)

            def body(c, with_group):
                if with_group:
                    load_group(c)
                for par in range(2):
                    sp.wait_ge(keys_free, 2 * c + par + 1)
                    sp.dma_start(keys[par][:, :], scr["keys"][:, bass.ds(c * PAIR + (par + 2) * ET, ET)])\
                        .then_inc(keys_in[par], 16)
                    if with_group:
                        for e in (2 * par, 2 * par + 1):
                            store_output(c, e)

            def group(g):
                load_group(g)
                for e in range(NX):
                    store_output(g, e)

            edge_loop(sp, body, group)
            for i in range(2):
                sp.wait_ge(y_stored[i], 16 + 16 * NFG * NX // 2)
            sp.wait_ge(done, 1)
            sp.dma_start(scr["gates"].rearrange("(t p) f -> p t f", p=P), gates[:, :, :]).then_inc(stored, 16)
            sp.wait_ge(stored, 16)

        @block.gpsimd
        def _(pool):
            make_identity(pool, ident, ident_ok)
            pool.iota(iota_i[:, :], pattern=[[1, HI]], base=0, channel_multiplier=0).then_inc(ident_ok, 1)
            pool.wait_ge(peak_ok, 1)
            pool.partition_all_reduce(peak[:, :], peak[:, :], P, REDUCE_MAX).then_inc(peak_all, 1)
            pool.wait_ge(limit_ok, 1)
            pool.partition_all_reduce(limits[:, 0:1], limits[:, 0:1], P, REDUCE_MAX).then_inc(limit_all, 1)
            pool.wait_ge(const_in, 96)
            pool.wait_ge(table_out, 16)

            def body(c, with_group):
                for par in range(2):
                    pool.wait_ge(decoded, 2 * c + par + 1)
                    pool.wait_ge(weight_ok, 2 * c + par + 1)
                    part_wait(pool, passed)
                    for t in range(ET):
                        pool.indirect_dma_start(g_src[par][:, t, :], None, scr["nodes"],
                                                bass.IndirectOffsetOnAxis(src_i[par][:, t:t + 1].bitcast(U32), 0))\
                            .then_inc(src_got[par], 16)
                        pool.indirect_dma_start(g_dst[par][:, t, :], None, scr["dst_table"],
                                                bass.IndirectOffsetOnAxis(dst_i[par][:, t:t + 1].bitcast(U32), 0))\
                            .then_inc(dst_got[par], 16)

            edge_loop(pool, body)

        @block.scalar
        def _(act):
            act.wait_ge(exp_in, 1)
            act.activation(loops[:, :, HF:], work[0][:, :, 0:GHD], ACT.Exp).then_inc(exp_out, 1)
            act.wait_ge(const_in, 96)
            act.wait_ge(weights_in, 16 * (CC + 2 * NX + 1))

            def gelu(g, e):
                act.wait_ge(y_done, g * NX + e + 1)
                for c in range(FC):
                    act.wait_ge(h_done, NX * FC + (g * NX + e) * FC + c + 1)
                    act.activation(hidden[:, c, :], h_ps[:, c, :FT], ACT.Gelu, bias=b1[:, e, c:c + 1])\
                        .then_inc(gelu_ok, 1)

            def body(c, with_group):
                for par in range(2):
                    act.wait_ge(logit_ok, 2 * c + par + 1)
                    act.activation(val[:, :, HF:], logit[:, :, :], ACT.Exp).then_inc(exp_out, 1)
                    if with_group:
                        for e in (2 * par, 2 * par + 1):
                            gelu(c, e)

            def group(g):
                for e in range(NX):
                    gelu(g, e)

            edge_loop(act, body, group)
            act.wait_ge(root_in, 1)
            act.activation(small[2][:, :], small[1][:, :], ACT.Sqrt, bias=eps[:, :]).then_inc(root_out, 1)
            act.wait_ge(root_in, 2)
            act.activation(gates[:, :, :], score[:, :, :], ACT.Exp).then_inc(root_out, 1)

        @block.tensor
        def _(pe):
            pe.wait_ge(ident_ok, 2)
            pe.wait_ge(table_ok, 1)
            pe.wait_ge(const_in, 96)
            pe.wait_ge(weights_in, 16 * (CC + 2 * NX + 1))
            pe.sem_inc(h_done, NX * FC)
            pe.sem_inc(y_done, 1)
            for n in range(3):
                pe.matmul(acc[:AROWS, n, :], zeros[:, 0:AROWS], zeros[:, :], start=True, stop=False, skip_group_check=True)

            def hide(g, e):
                if e == 0:
                    pe.wait_ge(t_in, 16 * g + 16)
                for c in range(FC):
                    for k in range(CC):
                        last = pe.matmul(h_ps[:, c, :FT], w1[:, k, e, c * P:(c + 1) * P], tT[:, k, :],
                                         start=(k == 0), stop=(k == CC - 1))
                    last.then_inc(h_done, 1)

            def output(g, e):
                pe.wait_ge(gelu_ok, (g * NX + e) * FC + FC)
                pe.wait_ge(y_taken, g * NX + e + 1)
                for t in range(FG):
                    for c in range(FC):
                        last = pe.matmul(y_ps[:, t, :], hidden[:, c, t * P:(t + 1) * P], w2[:, e, c, :],
                                         start=(c == 0), stop=(c == FC - 1))
                last.then_inc(y_done, 1)

            def group(g):
                for e in range(NX):
                    hide(g, e)
                    output(g, e)

            def edges(parts, dt):
                def body(c, with_group):
                    for par in range(2):
                        pe.wait_ge(spread_ok, 2 * c + par + 1)
                        for t in range(ET):
                            pe.wait_ge(one_ok, (2 * c + par) * ET + t + 1)
                            for k in range(parts):
                                weights = spread[par][k][:, t, :, :].rearrange("p l f -> p (l f)")
                                for n in range(3):
                                    last = pe.matmul(acc[:AROWS, n, :], weights.bitcast(dt),
                                                     one_hi[t % B_RING][:, n * 512:(n + 1) * 512].bitcast(dt),
                                                     start=False, stop=False, skip_group_check=True)
                            last.then_inc(tile_done, 1)
                            if with_group and t in HIDE_AT:
                                hide(c, 2 * par + HIDE_AT.index(t))
                            if with_group and t in OUT_AT:
                                output(c, 2 * par + OUT_AT.index(t))

                edge_loop(pe, body, group)

            by_range(pe, edges)
            for n in range(3):
                last = pe.matmul(acc[:AROWS, n, :], zeros[:, 0:AROWS], zeros[:, :], start=False, stop=True,
                                 skip_group_check=True)
            last.then_inc(acc_done, 1)

            pe.wait_ge(evac_ok, 1)
            pe.wait_ge(gelu_ok, NFG * NX * FC)
            for k in range(BLK):
                if k >= 4:
                    pe.wait_ge(block_taken, k - 3)
                pe.transpose(h_ps[:, k % 4, 0:AROWS], acc_sb[:, k * P:(k + 1) * P], ident[:AROWS, :AROWS])\
                    .then_inc(block_turned, 1)

        @block.vector
        def _(dve):
            step = Steps(dve, dve_s)

            def leaky(out, x):
                step(dve.scalar_tensor_tensor(out=out, in0=x, scalar=0.2, in1=x, op0=ALU.mult, op1=ALU.max))

            def over_heads(ap):
                return ap.rearrange("p t (h x) -> p t h x", x=NX)

            dve.wait_ge(const_in, 96)
            dve.wait_ge(ident_ok, 3)
            step(dve.memset(zeros[:, :], 0.0))
            step(dve.tensor_scalar(iota_hi[:, :], iota_i[:, :], 1.0, None, ALU.add))
            step(dve.tensor_copy(iota_f[:, :], iota_i[:, 0:ET]))
            step(dve.tensor_copy(left[:, :], counts[:, 1:2]))
            src_logit = nodes[:, :, HF:HF + GHD]
            dst_logit = nodes[:, :, HF + GHD:NF]
            dve.tensor_reduce(peak[:, :], src_logit.rearrange("p t h -> p h t"), AX.X, ALU.max).then_inc(peak_ok, 1)
            dve.wait_ge(peak_all, 1)
            high, own, tmp = dst_rows[:, :, GHD:], work[1][:, :, 0:GHD], work[0][:, :, 0:GHD]
            step(dve.tensor_tensor(tmp, dst_logit, peak[:, None, :].to_broadcast([P, NTILE, GHD]), ALU.add))
            leaky(high, tmp)
            step(dve.tensor_tensor(tmp, src_logit, dst_logit, ALU.add))
            leaky(own, tmp)
            step(dve.tensor_tensor(tmp, high, own, ALU.subtract))
            step(dve.tensor_reduce(limits[:, 0:1], tmp.rearrange("p t h -> p h t"), AX.XY, ALU.max))
            step(dve.scalar_tensor_tensor(out=high, in0=tmp, scalar=-0.5, in1=high, op0=ALU.mult, op1=ALU.add))
            step(dve.tensor_scalar(high, high, SCALE, None, ALU.subtract))
            step(dve.tensor_copy(dst_rows[:, :, 0:GHD], dst_logit))
            dve.sem_inc(table_ok, 1)
            step(dve.tensor_tensor(tmp, own, high, ALU.subtract))
            dve.sem_inc(exp_in, 1)
            step(dve.tensor_tensor(work[1][:, :, :], nodes[:, :, 0:HF], nodes[:, :, 0:HF], ALU.mult))
            step(dve.tensor_reduce(limits[:, 1:2], work[1][:, :, :], AX.XY, ALU.max))
            step(dve.tensor_scalar(limits[:, 1:2], limits[:, 1:2], RANGE / FEATURE ** 2, None, ALU.mult))
            step(dve.tensor_tensor(limits[:, 0:1], limits[:, 0:1], limits[:, 1:2], ALU.max))
            dve.sem_inc(limit_ok, 1)
            dve.wait_ge(limit_all, 1)
            step(dve.tensor_scalar(wide[:, :], limits[:, 0:1], RANGE, None, ALU.is_gt))
            dve.sem_inc(wide_ok, 1)
            dve.wait_ge(exp_out, 1)
            step(dve.tensor_tensor(over_heads(loops[:, :, 0:HF]), over_heads(nodes[:, :, 0:HF]),
                                   loops[:, :, HF:, None].to_broadcast([P, NTILE, GHD, NX]), ALU.mult))

            dve.sem_inc(weight_ok, 2)

            def indices(i, par):
                dve.wait_ge(keys_in[par], 16 * i + 16)
                step(dve.tensor_scalar(src_i[par][:, :], keys[par][:, :], (1 << SRC_BITS) - 1, None, ALU.bitwise_and))
                step(dve.tensor_scalar(dst_i[par][:, :], keys[par][:, :], SRC_BITS, None, ALU.logical_shift_right))
                dve.sem_inc(keys_free, 1)
                step(dve.tensor_scalar(inside[par][:, :], iota_f[:, :], left[:, 0:1], None, ALU.is_lt))
                step(dve.tensor_scalar(left[:, :], left[:, :], float(ET), None, ALU.subtract))
                step(dve.tensor_tensor(src_i[par][:, :], src_i[par][:, :], inside[par][:, :], ALU.mult))
                step(dve.tensor_tensor(dst_i[par][:, :], dst_i[par][:, :], inside[par][:, :], ALU.mult))
                dve.sem_inc(decoded, 1)

            def codes(par):
                step(dve.tensor_scalar(lo[:, :], dst_i[par][:, :], float(HI), None, ALU.is_ge))
                for j in range(2, LO):
                    step(dve.scalar_tensor_tensor(out=lo[:, :], in0=dst_i[par][:, :], scalar=float(j * HI),
                                                  in1=lo[:, :], op0=ALU.is_ge, op1=ALU.add))
                step(dve.scalar_tensor_tensor(out=hi[:, :], in0=lo[:, :], scalar=-float(HI),
                                              in1=dst_i[par][:, :], op0=ALU.mult, op1=ALU.add))
                step(dve.scalar_tensor_tensor(out=hi[:, :], in0=hi[:, :], scalar=1.0,
                                              in1=inside[par][:, :], op0=ALU.add, op1=ALU.mult))

            def take_output(g, e):
                dve.wait_ge(y_stored[e % 2], 16 + 16 * (g * (NX // 2) + e // 2))
                dve.wait_ge(y_done, 1 + g * NX + e + 1)
                dve.tensor_tensor(y[e % 2][:, :, :], y_ps[:, :, :],
                                  b2_row[:, e, None, :].to_broadcast([P, FG, C]), ALU.add).then_inc(y_taken, 1)

            def process(n, i, par, parts, dt, g):
                lo_code = one_lo[:, :, :].bitcast(dt)
                pieces = [part[k][:, :, :].bitcast(dt) for k in range(parts)]
                codes(par)
                step(dve.tensor_tensor(lo_code, lo[:, :, None].to_broadcast([P, ET, LO]),
                                       iota_f[:, None, 0:LO].to_broadcast([P, ET, LO]), ALU.is_equal))
                dve.wait_ge(src_got[par], 16 * ET * (i + 1))
                dve.wait_ge(dst_got[par], 16 * ET * (i + 1))
                step(dve.tensor_tensor(logit[:, :, :], g_src[par][:, :, HF:HF + GHD], g_dst[par][:, :, 0:GHD], ALU.add))
                leaky(logit2[:, :, :], logit[:, :, :])
                step(dve.tensor_tensor(logit[:, :, :], logit2[:, :, :], g_dst[par][:, :, GHD:], ALU.subtract))
                dve.sem_inc(logit_ok, 1)
                dve.wait_ge(exp_out, n + 2)
                step(dve.tensor_tensor(over_heads(val[:, :, 0:HF]), over_heads(g_src[par][:, :, 0:HF]),
                                       val[:, :, HF:, None].to_broadcast([P, ET, GHD, NX]), ALU.mult))
                dve.sem_inc(weight_ok, 1)
                whole = val
                for k in range(parts - 1):
                    step(dve.tensor_copy(pieces[k], whole[:, :, :]))
                    last = k == parts - 2
                    step(dve.tensor_tensor(pieces[k + 1] if last else rest[:, :, :], whole[:, :, :], pieces[k],
                                           ALU.subtract))
                    whole = rest
                dve.wait_ge(tile_done, ET * (n + 1))
                for k in range(parts):
                    step(dve.tensor_tensor(spread[par][k][:, :, :, :].bitcast(dt),
                                           lo_code[:, :, :, None].to_broadcast([P, ET, LO, TR]),
                                           pieces[k][:, :, None, :].to_broadcast([P, ET, LO, TR]), ALU.mult))
                dve.sem_inc(spread_ok, 1)
                for t in range(ET):
                    if t == INDEX_AT:
                        indices(i + 1, par)
                    dve.wait_ge(tile_done, ET * n + t + 2 * ET - B_RING + 1)
                    dve.tensor_scalar(one_hi[t % B_RING][:, :].bitcast(dt), iota_hi[:, :], hi[:, t:t + 1], None,
                                      ALU.is_equal).then_inc(one_ok, 1)
                    if g is not None and t in TAKE_AT:
                        take_output(g, 2 * par + TAKE_AT.index(t))

            dve.sem_inc(tile_done, 2 * ET)
            indices(0, 0)
            indices(0, 1)
            dve.wait_ge(weights_in, 16 * (CC + 2 * NX + 1))
            dve.sem_inc(y_taken, 1)
            before_loop = step.n

            def group(g):
                for e in range(NX):
                    take_output(g, e)

            def edges(parts, dt):
                per = 2 * (13 + 5 + 2 * (parts - 1) + parts)

                def body(c, with_group):
                    step.start, step.n = before_loop + c * per, 0
                    for par in range(2):
                        process(2 * c + par, c, par, parts, dt, c if with_group else None)
                    assert step.n == per, (step.n, per)

                edge_loop(dve, body, group)

            by_range(dve, edges)

            step = Steps(dve, tail_s)
            dve.wait_ge(acc_done, 1)
            dve.tensor_copy(acc_sb[:, :].rearrange("p (n c) -> p n c", n=3), acc[:AROWS, :, :]).then_inc(evac_ok, 1)
            for k in range(BLK):
                dve.wait_ge(block_turned, k + 1)
                dve.tensor_copy(sums[:, k:NTILE:BLK, :], h_ps[:, k % 4, 0:AROWS].rearrange("p (l f) -> p l f", l=LO))\
                    .then_inc(block_taken, 1)
            dve.wait_ge(block_taken, BLK)
            step(dve.tensor_tensor(sums[:, :, :], sums[:, :, :], loops[:, :, :], ALU.add))
            step(dve.reciprocal(sums[:, :, HF:], sums[:, :, HF:]))
            agg, square = work
            step(dve.tensor_tensor(over_heads(agg[:, :, :]), over_heads(sums[:, :, 0:HF]),
                                   sums[:, :, HF:, None].to_broadcast([P, NTILE, GHD, NX]), ALU.mult))

            def row(ap):
                return ap[:, None, :].to_broadcast([P, NTILE, HF])

            def col(ap, n):
                return ap[:, :, None].to_broadcast([P, NTILE, n])

            step(dve.tensor_tensor(agg[:, :, :], agg[:, :, :], row(b_gat), ALU.add))
            step(dve.tensor_reduce(small[0][:, :], agg[:, :, :], AX.X, ALU.add))
            step(dve.tensor_scalar(small[0][:, :], small[0][:, :], 1.0 / HF, None, ALU.mult))
            step(dve.tensor_tensor(agg[:, :, :], agg[:, :, :], col(small[0], HF), ALU.subtract))
            step(dve.tensor_tensor(square[:, :, :], agg[:, :, :], agg[:, :, :], ALU.mult))
            step(dve.tensor_reduce(small[1][:, :], square[:, :, :], AX.X, ALU.add))
            step(dve.tensor_scalar(small[1][:, :], small[1][:, :], 1.0 / HF, None, ALU.mult))
            dve.sem_inc(root_in, 1)
            dve.wait_ge(root_out, 1)
            reciprocal_root(dve, step, small[2], small[1][:, :], small[3], LN_EPS)
            step(dve.tensor_tensor(agg[:, :, :], agg[:, :, :], col(small[2], HF), ALU.mult))
            step(dve.tensor_tensor(agg[:, :, :], agg[:, :, :], row(gamma), ALU.mult))
            step(dve.tensor_tensor(agg[:, :, :], agg[:, :, :], row(beta), ALU.add))
            step(dve.tensor_reduce(score[:, :, :], agg[:, :, :].rearrange("p t (h x) -> p t x h", x=NX), AX.X, ALU.add))
            step(dve.tensor_scalar(score[:, :, :], score[:, :, :], 1.0 / GHD, None, ALU.mult))
            for i in range(NX):
                step(dve.memset(rank[:, :, i], float(NX - 1 - i)))
            for i in range(NX):
                for j in range(i + 1, NX):
                    step(dve.tensor_tensor(small[0][:, :], score[:, :, i], score[:, :, j], ALU.is_ge))
                    step(dve.tensor_tensor(rank[:, :, j], rank[:, :, j], small[0][:, :], ALU.add))
                    step(dve.tensor_tensor(rank[:, :, i], rank[:, :, i], small[0][:, :], ALU.subtract))
            step(dve.tensor_reduce(small[0][:, :], score[:, :, :], AX.X, ALU.max))
            step(dve.tensor_tensor(score[:, :, :], score[:, :, :], col(small[0], NX), ALU.subtract))
            step(dve.tensor_scalar(rank[:, :, :], rank[:, :, :], 1.5, None, ALU.is_lt))
            dve.sem_inc(root_in, 1)
            dve.wait_ge(root_out, 2)
            step(dve.tensor_tensor(gates[:, :, :], gates[:, :, :], rank[:, :, :], ALU.mult))
            step(dve.tensor_reduce(small[0][:, :], gates[:, :, :], AX.X, ALU.add))
            step(dve.reciprocal(small[0][:, :], small[0][:, :]))
            step(dve.tensor_tensor(gates[:, :, :], gates[:, :, :], col(small[0], NX), ALU.mult))
            dve.sem_inc(done, 1)


def combine(nc, scr, out):
    RING = 4
    ctx = ExitStack()
    with ctx:
        s = Space(nc, ctx, "sum")
        y = [s.sb(f"y{i}", [P, NX, FG, C]) for i in range(RING)]
        total = [s.sb(f"total{i}", [P, FG, C]) for i in range(RING)]
        gates = s.sb("gates", [P, NTILE, NX])
        gates_in = s.sem("gates_in")
        in_ready = [s.sem(f"in_ready{i}") for i in range(RING)]
        total_ok = s.sem("total_ok")
        stored = [s.sem(f"stored{i}") for i in range(RING)]
        dve_s = s.sem("dve_s")
        x2_v = scr["x2"].rearrange("(g t p) c -> g p t c", t=FG, p=P)
        out_v = out.rearrange("(g t p) c -> g p t c", t=FG, p=P)
        y_v = scr["y"].rearrange("g x p (t c) -> g p x t c", t=FG)
        block = ctx.enter_context(nc.Block())

        @block.sync
        def _(sp):
            sp.dma_start(gates[:, :, :], scr["gates"].rearrange("(t p) f -> p t f", p=P)).then_inc(gates_in, 16)
            for r in range(RING):
                sp.sem_inc(stored[r], 16)
            with sp.Fori(0, NFG // RING) as i:
                for r in range(RING):
                    sp.wait_ge(stored[r], 16 + 16 * i)
                    sp.dma_start(y[r][:, :, :, :], y_v[i * RING + r]).then_inc(in_ready[r], 16)
                    sp.dma_start(total[r][:, :, :], x2_v[i * RING + r]).then_inc(in_ready[r], 16)

        @block.scalar
        def _(act):
            with act.Fori(0, NFG // RING) as i:
                for r in range(RING):
                    act.wait_ge(total_ok, i * RING + r + 1)
                    act.dma_start(out_v[i * RING + r], total[r][:, :, :]).then_inc(stored[r], 16)
            for r in range(RING):
                act.wait_ge(stored[r], 16 + 16 * NFG // RING)

        @block.vector
        def _(dve):
            step = Steps(dve, dve_s)
            dve.wait_ge(gates_in, 16)
            with dve.Fori(0, NFG // RING) as i:
                for r in range(RING):
                    g = i * RING + r
                    step.start, step.n = g * NX * FG, 0
                    dve.wait_ge(in_ready[r], 32 * i + 32)
                    for e in range(NX):
                        for t in range(FG):
                            step(dve.scalar_tensor_tensor(
                                out=total[r][:, t, :], in0=y[r][:, e, t, :],
                                scalar=gates[:, bass.ds(g * FG + t, 1), e], in1=total[r][:, t, :],
                                op0=ALU.mult, op1=ALU.add), lag=FG - 1)
                    step.wait()
                    dve.sem_inc(total_ok, 1)


_OUT = (B, H, W, C)


def layouts(i):
    conv = {n: i["L0_conv_" + n] for n in
            ("sin", "cos", "mask", "Wq", "bq", "Wk", "bk", "Wv", "bv", "dw_w", "dw_b", "Wo", "bo")}
    ffn = {n: i["L0_ffn_" + n] for n in
           ("W_gat", "att_src", "att_dst", "b_gat", "ln_gamma", "ln_beta", "W1", "b1", "W2", "b2")}
    swap = np.arange(C) ^ 1

    def column(v):
        return v.reshape(CC, P).T

    return {
        "x": i["x"].reshape(M, C),
        "Wq": conv["Wq"], "Wq_swap": conv["Wq"][:, swap], "Wk": conv["Wk"], "Wk_swap": conv["Wk"][:, swap],
        "Wv": conv["Wv"], "Wo": conv["Wo"],
        "bq": column(conv["bq"]), "bq_swap": column(conv["bq"][swap]),
        "bk": column(conv["bk"]), "bk_swap": column(conv["bk"][swap]),
        "bv": column(conv["bv"]), "bv_row": conv["bv"].reshape(1, C), "bo_row": conv["bo"].reshape(1, C),
        "cos": conv["cos"].reshape(N, HD).T, "sin": conv["sin"].reshape(N, HD).T,
        "sign": np.where(np.arange(P) % 2 == 0, -1.0, 1.0).astype(np.float32).reshape(P, 1),
        "ln_eps": np.full((1, 1), LN_EPS, np.float32),
        "mask": conv["mask"],
        "dw_w": conv["dw_w"].reshape(25, CC, P).transpose(2, 1, 0), "dw_b": column(conv["dw_b"]),
        "W_gat": ffn["W_gat"], "att_src": ffn["att_src"].reshape(1, HF), "att_dst": ffn["att_dst"].reshape(1, HF),
        "b_gat": ffn["b_gat"].reshape(1, HF), "ln_gamma": ffn["ln_gamma"].reshape(1, HF),
        "ln_beta": ffn["ln_beta"].reshape(1, HF),
        "W1": ffn["W1"], "b1": ffn["b1"].reshape(NX, GF // P, P).transpose(2, 0, 1), "W2": ffn["W2"], "b2": ffn["b2"],
        "edges": i["L0_ffn_edge_index"],
    }


def metaformer(nc, a, out):
    shapes = {
        "q_parts": ((NH, 4 * HD, M), F16), "k_parts": ((NH, 4 * HD, M), F16),
        "v_stack": ((B, NH, P, JM * VS), F16), "v_pad": ((C, B, PH * PW), F32),
        "att": ((2, C, M), F32), "att_sum": ((NH, M), F32), "denom": ((NH, M), F32),
        "x2": ((M, C), F32), "tT": ((C, M), F32),
        "nodes": ((M, HF + 2 * GHD), F32), "dst_table": ((M, 2 * GHD), F32),
        "keys": ((P, EC + PAIR), I32), "counts": ((P, 2), I32), "gates": ((M, NX), F32),
        "y": ((NFG, NX, P, FG * C), F32),
    }
    scr = {n: nc.dram_tensor(f"scr_{n}", shape, dt, kind="Internal").ap() for n, (shape, dt) in shapes.items()}
    project_and_pack(nc, a, scr)
    attend(nc, a, scr)
    mix_and_normalise(nc, a, scr)
    aggregate(nc, a, scr)
    combine(nc, scr, out)


def kernel(**inputs):
    import concourse.bacc as bacc
    from concourse.bass_utils import run_bass_kernel_spmd

    nc = bacc.Bacc("TRN2", target_bir_lowering=False, num_devices=1)
    arrays, aps = {}, {}
    for name, v in layouts({n: np.asarray(v) for n, v in inputs.items()}).items():
        v = np.ascontiguousarray(v)
        arrays[f"in_{name}"] = v
        aps[name] = nc.dram_tensor(f"in_{name}", v.shape, mybir.dt.from_np(v.dtype), kind="ExternalInput").ap()
    out = nc.dram_tensor("out", (M, C), F32, kind="ExternalOutput").ap()
    metaformer(nc, aps, out)
    r = run_bass_kernel_spmd(nc, [arrays], core_ids=[0])
    return r.results[0]["out"].reshape(_OUT)
```
